# Optimizing a Trainium2 kernel written in Bass

```python
import numpy as np
import jax
import jax.numpy as jnp

def _softmax(x, axis=-1):
    return jax.nn.softmax(x, axis=axis)

def _gelu(x):
    return jax.nn.gelu(x, approximate=True)

def _silu(x):
    return jax.nn.silu(x)

def _sigmoid(x):
    return jax.nn.sigmoid(x)

def _layernorm(x, axis=-1, eps=1e-05):
    m = jnp.mean(x, axis=axis, keepdims=True)
    v = jnp.var(x, axis=axis, keepdims=True)
    return (x - m) / jnp.sqrt(v + eps)

def _scatter_add(tgt, idx, src, axis=0):
    return tgt.at[idx].add(src)

def _segment_sum(src, seg, n):
    return jax.ops.segment_sum(src, seg, n)
kernel_name = 'mk_macaron_d4_jaxref_r8_6fdff7'

def setup_inputs(seed: int=0):
    np.random.seed(seed)
    _w = jnp.asarray

    def _L0_attn_setup():
        import jax, jax.numpy as jnp
        import numpy as np
        B, L, D1, D2, N = (4, 256, 128, 128, 512)
        key = jax.random.key(seed)
        k1, k2, k3 = jax.random.split(key, 3)
        inputs = jax.random.normal(k1, (B, L, D1), dtype=jnp.float32)
        key_param_tokens = jax.random.normal(k2, (N, D1), dtype=jnp.float32) * 0.02
        value_param_tokens = jax.random.normal(k3, (N, D2), dtype=jnp.float32) * 0.02
        return {'inputs': inputs, 'key_param_tokens': key_param_tokens, 'value_param_tokens': value_param_tokens}
    _L0_attn_in = _L0_attn_setup()

    def _L0_ffn_setup():
        import jax, jax.numpy as jnp
        import numpy as np
        S, B, H, F, E, K = (256, 2, 128, 256, 8, 2)

        def _moe_forward(hidden_states, router_w, w1, b1, w2, b2):
            s, b, h = hidden_states.shape
            T = s * b
            x = hidden_states.reshape(T, h)
            logits = jnp.einsum('th,eh->te', x, router_w)
            topk_logits, topk_idx = jax.lax.top_k(logits, K)
            probs = jax.nn.softmax(topk_logits, axis=-1)
            combine = jnp.zeros((T, E), dtype=x.dtype)
            combine = combine.at[jnp.arange(T)[:, None], topk_idx].add(probs.astype(x.dtype))
            hmid = jnp.einsum('th,efh->etf', x, w1) + b1[:, None, :]
            hmid = jax.nn.gelu(hmid, approximate=False)
            y = jnp.einsum('etf,ehf->eth', hmid, w2) + b2[:, None, :]
            out = jnp.einsum('eth,te->th', y, combine)
            return out.reshape(s, b, h)
        key = jax.random.key(seed)
        ks = jax.random.split(key, 6)
        std = 0.02
        return {'hidden_states': jax.random.normal(ks[0], (S, B, H), dtype=jnp.float32), 'router_w': jax.random.normal(ks[1], (E, H), dtype=jnp.float32) * std, 'w1': jax.random.normal(ks[2], (E, F, H), dtype=jnp.float32) * (1.0 / np.sqrt(H)), 'b1': jnp.zeros((E, F), dtype=jnp.float32), 'w2': jax.random.normal(ks[3], (E, H, F), dtype=jnp.float32) * (1.0 / np.sqrt(F)), 'b2': jnp.zeros((E, H), dtype=jnp.float32)}
    _L0_ffn_in = _L0_ffn_setup()

    def _L1_attn_setup():
        import jax, jax.numpy as jnp
        import numpy as np
        N_EMBD = 128
        N_HEAD = 16
        HEAD = N_EMBD // N_HEAD
        key = jax.random.key(seed)
        ks = jax.random.split(key, 9)
        B, T, C = (2, 256, N_EMBD)
        s = 1.0 / np.sqrt(C)
        return {'x': jax.random.normal(ks[0], (B, T, C), dtype=jnp.float32), 'Wq': jax.random.normal(ks[1], (C, C), dtype=jnp.float32) * s, 'bq': jnp.zeros((C,), dtype=jnp.float32), 'Wk': jax.random.normal(ks[2], (C, C), dtype=jnp.float32) * s, 'bk': jnp.zeros((C,), dtype=jnp.float32), 'Wv': jax.random.normal(ks[3], (C, C), dtype=jnp.float32) * s, 'bv': jnp.zeros((C,), dtype=jnp.float32), 'Wo': jax.random.normal(ks[4], (C, C), dtype=jnp.float32) * s, 'bo': jnp.zeros((C,), dtype=jnp.float32)}
    _L1_attn_in = _L1_attn_setup()

    def _L1_ffn_setup():
        import jax, jax.numpy as jnp
        import numpy as np
        B, S, D, FF, E, TOP_K = (4, 256, 128, 512, 8, 2)

        def _hybrid_moe(x, Wr, br, Wg, bg, W1, b1, W2, b2, D1, d1b, D2, d2b):
            b, s, d = x.shape
            t = x.reshape(-1, d)
            T = t.shape[0]
            rp = jax.nn.softmax(x @ Wr + br, axis=-1)
            gp = jax.nn.softmax(t @ Wg + bg, axis=-1)
            vals, idx = jax.lax.top_k(gp, TOP_K)
            vals = vals / jnp.sum(vals, axis=-1, keepdims=True)
            cw = jnp.zeros((T, E), t.dtype).at[jnp.arange(T)[:, None], idx].add(vals)
            h = jax.nn.relu(jnp.einsum('td,edf->tef', t, W1) + b1)
            eo = jnp.einsum('tef,efd->ted', h, W2) + b2
            moe = jnp.einsum('te,ted->td', cw, eo).reshape(b, s, d)
            dense = jax.nn.relu(x @ D1 + d1b) @ D2 + d2b
            return rp[..., 0:1] * moe + rp[..., 1:2] * dense
        key = jax.random.key(seed)
        ks = jax.random.split(key, 13)
        sd = 1.0 / np.sqrt(D)
        sf = 1.0 / np.sqrt(FF)
        return {'x': jax.random.normal(ks[0], (B, S, D), jnp.float32), 'Wr': jax.random.normal(ks[1], (D, 2), jnp.float32) * sd, 'br': jnp.zeros((2,), jnp.float32), 'Wg': jax.random.normal(ks[2], (D, E), jnp.float32) * sd, 'bg': jnp.zeros((E,), jnp.float32), 'W1': jax.random.normal(ks[3], (E, D, FF), jnp.float32) * sd, 'b1': jnp.zeros((E, FF), jnp.float32), 'W2': jax.random.normal(ks[4], (E, FF, D), jnp.float32) * sf, 'b2': jnp.zeros((E, D), jnp.float32), 'D1': jax.random.normal(ks[5], (D, FF), jnp.float32) * sd, 'd1b': jnp.zeros((FF,), jnp.float32), 'D2': jax.random.normal(ks[6], (FF, D), jnp.float32) * sf, 'd2b': jnp.zeros((D,), jnp.float32)}
    _L1_ffn_in = _L1_ffn_setup()

    def _L2_attn_setup():
        import jax, jax.numpy as jnp
        import numpy as np
        B, S, D = (4, 256, 128)
        DK, DV = (128, 128)
        key = jax.random.key(seed)
        ks = jax.random.split(key, 5)
        x = jax.random.normal(ks[0], (B, S, D), dtype=jnp.float32)
        scale = 1.0 / np.sqrt(D)
        Wq = jax.random.normal(ks[1], (D, DK), dtype=jnp.float32) * scale
        Wk = jax.random.normal(ks[2], (D, DK), dtype=jnp.float32) * scale
        Wv = jax.random.normal(ks[3], (D, DV), dtype=jnp.float32) * scale
        Wo = jax.random.normal(ks[4], (DV, DV), dtype=jnp.float32) * (1.0 / np.sqrt(DV))
        return {'x': x, 'Wq': Wq, 'Wk': Wk, 'Wv': Wv, 'Wo': Wo}
    _L2_attn_in = _L2_attn_setup()

    def _L2_ffn_setup():
        import jax, jax.numpy as jnp
        import numpy as np
        from jax import lax
        TOP_K = 4
        N_GROUP = 4
        TOPK_GROUP = 2
        ROUTED_SCALE = 2.5
        NEG_INF = -1000000000.0

        def _route(xf, router_weight, router_bias):
            T = xf.shape[0]
            E = router_weight.shape[0]
            logits = xf @ router_weight.T
            scores = jax.nn.sigmoid(logits)
            s_choice = scores + router_bias
            per_group = E // N_GROUP
            sg = s_choice.reshape(T, N_GROUP, per_group)
            group_scores = lax.top_k(sg, 2)[0].sum(-1)
            _, gidx = lax.top_k(group_scores, TOPK_GROUP)
            gmask = jnp.zeros((T, N_GROUP), dtype=bool).at[jnp.arange(T)[:, None], gidx].set(True)
            masked = jnp.where(gmask[:, :, None], sg, NEG_INF).reshape(T, E)
            _, topk_idx = lax.top_k(masked, TOP_K)
            w = jnp.take_along_axis(scores, topk_idx, axis=1)
            w = w / (w.sum(-1, keepdims=True) + 1e-20) * ROUTED_SCALE
            combine = jnp.zeros((T, E), dtype=xf.dtype).at[jnp.arange(T)[:, None], topk_idx].add(w)
            return combine
        key = jax.random.key(seed)
        ks = jax.random.split(key, 6)
        B, S, H, I, E = (2, 256, 128, 64, 16)
        x = jax.random.normal(ks[0], (B, S, H), dtype=jnp.float32)
        router_weight = jax.random.normal(ks[1], (E, H), dtype=jnp.float32) * 0.02
        router_bias = jnp.zeros((E,), dtype=jnp.float32)
        w_gate = jax.random.normal(ks[2], (E, I, H), dtype=jnp.float32) * 0.02
        w_up = jax.random.normal(ks[3], (E, I, H), dtype=jnp.float32) * 0.02
        w_down = jax.random.normal(ks[4], (E, H, I), dtype=jnp.float32) * 0.02
        return {'x': x, 'router_weight': router_weight, 'router_bias': router_bias, 'w_gate': w_gate, 'w_up': w_up, 'w_down': w_down}
    _L2_ffn_in = _L2_ffn_setup()

    def _L3_attn_setup():
        import jax, jax.numpy as jnp
        import numpy as np
        GAMMA = 0.96875
        key = jax.random.key(seed)
        kx, kq, kk, kv = jax.random.split(key, 4)
        B, T, D = (4, 256, 128)
        x = jax.random.normal(kx, (B, T, D), dtype=jnp.float32)
        Wq = jax.random.normal(kq, (D, D), dtype=jnp.float32) * (1.0 / np.sqrt(D))
        Wk = jax.random.normal(kk, (D, D), dtype=jnp.float32) * (1.0 / np.sqrt(D))
        Wv = jax.random.normal(kv, (D, D), dtype=jnp.float32) * (1.0 / np.sqrt(D))
        return {'x': x, 'Wq': Wq, 'Wk': Wk, 'Wv': Wv}
    _L3_attn_in = _L3_attn_setup()

    def _L3_ffn_setup():
        import jax, jax.numpy as jnp
        import numpy as np
        EMB = 128
        FF = 4 * EMB

        def _ternary(w):
            scale = jnp.maximum(jnp.mean(jnp.abs(w)), 1e-08)
            w_t = jnp.clip(jnp.round(w / scale), -1.0, 1.0)
            return w + jax.lax.stop_gradient(w_t - w)
        key = jax.random.key(seed)
        kx, k1, k2, kb1, kb2 = jax.random.split(key, 5)
        x = jax.random.normal(kx, (4, 256, EMB), dtype=jnp.float32)
        lim1 = 1.0 / np.sqrt(EMB)
        lim2 = 1.0 / np.sqrt(FF)
        W1 = jax.random.uniform(k1, (FF, EMB), jnp.float32, -lim1, lim1)
        b1 = jax.random.uniform(kb1, (FF,), jnp.float32, -lim1, lim1)
        W2 = jax.random.uniform(k2, (EMB, FF), jnp.float32, -lim2, lim2)
        b2 = jax.random.uniform(kb2, (EMB,), jnp.float32, -lim2, lim2)
        return {'x': x, 'W1': W1, 'b1': b1, 'W2': W2, 'b2': b2}
    _L3_ffn_in = _L3_ffn_setup()
    _d = {'L0_attn_inputs': _L0_attn_in['inputs'], 'L0_attn_key_param_tokens': _L0_attn_in['key_param_tokens'], 'L0_attn_value_param_tokens': _L0_attn_in['value_param_tokens'], 'L0_ffn_router_w': _L0_ffn_in['router_w'], 'L0_ffn_w1': _L0_ffn_in['w1'], 'L0_ffn_b1': _L0_ffn_in['b1'], 'L0_ffn_w2': _L0_ffn_in['w2'], 'L0_ffn_b2': _L0_ffn_in['b2'], 'L1_attn_Wq': _L1_attn_in['Wq'], 'L1_attn_bq': _L1_attn_in['bq'], 'L1_attn_Wk': _L1_attn_in['Wk'], 'L1_attn_bk': _L1_attn_in['bk'], 'L1_attn_Wv': _L1_attn_in['Wv'], 'L1_attn_bv': _L1_attn_in['bv'], 'L1_attn_Wo': _L1_attn_in['Wo'], 'L1_attn_bo': _L1_attn_in['bo'], 'L1_ffn_Wr': _L1_ffn_in['Wr'], 'L1_ffn_br': _L1_ffn_in['br'], 'L1_ffn_Wg': _L1_ffn_in['Wg'], 'L1_ffn_bg': _L1_ffn_in['bg'], 'L1_ffn_W1': _L1_ffn_in['W1'], 'L1_ffn_b1': _L1_ffn_in['b1'], 'L1_ffn_W2': _L1_ffn_in['W2'], 'L1_ffn_b2': _L1_ffn_in['b2'], 'L1_ffn_D1': _L1_ffn_in['D1'], 'L1_ffn_d1b': _L1_ffn_in['d1b'], 'L1_ffn_D2': _L1_ffn_in['D2'], 'L1_ffn_d2b': _L1_ffn_in['d2b'], 'L2_attn_Wq': _L2_attn_in['Wq'], 'L2_attn_Wk': _L2_attn_in['Wk'], 'L2_attn_Wv': _L2_attn_in['Wv'], 'L2_attn_Wo': _L2_attn_in['Wo'], 'L2_ffn_router_weight': _L2_ffn_in['router_weight'], 'L2_ffn_router_bias': _L2_ffn_in['router_bias'], 'L2_ffn_w_gate': _L2_ffn_in['w_gate'], 'L2_ffn_w_up': _L2_ffn_in['w_up'], 'L2_ffn_w_down': _L2_ffn_in['w_down'], 'L3_attn_Wq': _L3_attn_in['Wq'], 'L3_attn_Wk': _L3_attn_in['Wk'], 'L3_attn_Wv': _L3_attn_in['Wv'], 'L3_ffn_W1': _L3_ffn_in['W1'], 'L3_ffn_b1': _L3_ffn_in['b1'], 'L3_ffn_W2': _L3_ffn_in['W2'], 'L3_ffn_b2': _L3_ffn_in['b2']}
    _x0 = _d['L0_attn_inputs']
    _d['L0_attn_inputs'] = jax.random.normal(jax.random.fold_in(jax.random.key(seed), 1), (16, 256, 128), dtype=_x0.dtype)
    del _x0
    return _d

def reference(L0_attn_inputs, L0_attn_key_param_tokens, L0_attn_value_param_tokens, L0_ffn_router_w, L0_ffn_w1, L0_ffn_b1, L0_ffn_w2, L0_ffn_b2, L1_attn_Wq, L1_attn_bq, L1_attn_Wk, L1_attn_bk, L1_attn_Wv, L1_attn_bv, L1_attn_Wo, L1_attn_bo, L1_ffn_Wr, L1_ffn_br, L1_ffn_Wg, L1_ffn_bg, L1_ffn_W1, L1_ffn_b1, L1_ffn_W2, L1_ffn_b2, L1_ffn_D1, L1_ffn_d1b, L1_ffn_D2, L1_ffn_d2b, L2_attn_Wq, L2_attn_Wk, L2_attn_Wv, L2_attn_Wo, L2_ffn_router_weight, L2_ffn_router_bias, L2_ffn_w_gate, L2_ffn_w_up, L2_ffn_w_down, L3_attn_Wq, L3_attn_Wk, L3_attn_Wv, L3_ffn_W1, L3_ffn_b1, L3_ffn_W2, L3_ffn_b2):

    def _L0_attn_ref(inputs, key_param_tokens, value_param_tokens):
        import jax, jax.numpy as jnp
        import numpy as np
        B, L, D1, D2, N = (4, 256, 128, 128, 512)
        attn_weight = jnp.einsum('bld,nd->bln', inputs, key_param_tokens)
        n = attn_weight.shape[-1]
        l2 = jnp.sqrt(jnp.sum(attn_weight * attn_weight, axis=-1, keepdims=True))
        normed = attn_weight / l2 * jnp.sqrt(jnp.asarray(n, attn_weight.dtype))
        attn_weight = jax.nn.gelu(normed, approximate=False)
        return jnp.einsum('bln,nd->bld', attn_weight, value_param_tokens)

    def _L0_ffn_ref(hidden_states, router_w, w1, b1, w2, b2):
        import jax, jax.numpy as jnp
        import numpy as np
        S, B, H, F, E, K = (256, 2, 128, 256, 8, 2)

        def _moe_forward(hidden_states, router_w, w1, b1, w2, b2):
            s, b, h = hidden_states.shape
            T = s * b
            x = hidden_states.reshape(T, h)
            logits = jnp.einsum('th,eh->te', x, router_w)
            topk_logits, topk_idx = jax.lax.top_k(logits, K)
            probs = jax.nn.softmax(topk_logits, axis=-1)
            combine = jnp.zeros((T, E), dtype=x.dtype)
            combine = combine.at[jnp.arange(T)[:, None], topk_idx].add(probs.astype(x.dtype))
            hmid = jnp.einsum('th,efh->etf', x, w1) + b1[:, None, :]
            hmid = jax.nn.gelu(hmid, approximate=False)
            y = jnp.einsum('etf,ehf->eth', hmid, w2) + b2[:, None, :]
            out = jnp.einsum('eth,te->th', y, combine)
            return out.reshape(s, b, h)
        return _moe_forward(hidden_states, router_w, w1, b1, w2, b2)

    def _L1_attn_ref(x, Wq, bq, Wk, bk, Wv, bv, Wo, bo):
        import jax, jax.numpy as jnp
        import numpy as np
        N_EMBD = 128
        N_HEAD = 16
        HEAD = N_EMBD // N_HEAD
        B, T, C = x.shape

        def split(h):
            return h.reshape(B, T, N_HEAD, HEAD).transpose(0, 2, 1, 3)
        q = split(x @ Wq.T + bq)
        k = split(x @ Wk.T + bk)
        v = split(x @ Wv.T + bv)
        att = jnp.einsum('bhqd,bhkd->bhqk', q, k) * HEAD ** (-0.5)
        causal = jnp.tril(jnp.ones((T, T), dtype=bool))
        att = jnp.where(causal, att, -jnp.inf)
        att = jax.nn.softmax(att, axis=-1)
        y = jnp.einsum('bhqk,bhkd->bhqd', att, v)
        y = y.transpose(0, 2, 1, 3).reshape(B, T, C)
        return y @ Wo.T + bo

    def _L1_ffn_ref(x, Wr, br, Wg, bg, W1, b1, W2, b2, D1, d1b, D2, d2b):
        import jax, jax.numpy as jnp
        import numpy as np
        B, S, D, FF, E, TOP_K = (4, 256, 128, 512, 8, 2)

        def _hybrid_moe(x, Wr, br, Wg, bg, W1, b1, W2, b2, D1, d1b, D2, d2b):
            b, s, d = x.shape
            t = x.reshape(-1, d)
            T = t.shape[0]
            rp = jax.nn.softmax(x @ Wr + br, axis=-1)
            gp = jax.nn.softmax(t @ Wg + bg, axis=-1)
            vals, idx = jax.lax.top_k(gp, TOP_K)
            vals = vals / jnp.sum(vals, axis=-1, keepdims=True)
            cw = jnp.zeros((T, E), t.dtype).at[jnp.arange(T)[:, None], idx].add(vals)
            h = jax.nn.relu(jnp.einsum('td,edf->tef', t, W1) + b1)
            eo = jnp.einsum('tef,efd->ted', h, W2) + b2
            moe = jnp.einsum('te,ted->td', cw, eo).reshape(b, s, d)
            dense = jax.nn.relu(x @ D1 + d1b) @ D2 + d2b
            return rp[..., 0:1] * moe + rp[..., 1:2] * dense
        return _hybrid_moe(x, Wr, br, Wg, bg, W1, b1, W2, b2, D1, d1b, D2, d2b)

    def _L2_attn_ref(x, Wq, Wk, Wv, Wo):
        import jax, jax.numpy as jnp
        import numpy as np
        B, S, D = (4, 256, 128)
        DK, DV = (128, 128)
        dim_k = Wq.shape[1]
        q = x @ Wq
        k = x @ Wk
        v = x @ Wv
        scores = jnp.einsum('bsd,btd->bst', q, k)
        m_inf = -jnp.finfo(scores.dtype).max
        causal_mask = jnp.triu(jnp.ones((q.shape[1], q.shape[1]), dtype=bool), k=1)
        scores = jnp.where(causal_mask[None, :, :], m_inf, scores)
        attn = jax.nn.softmax(scores * dim_k ** (-0.5), axis=-1)
        out = jnp.einsum('bst,btv->bsv', attn, v) @ Wo
        return out

    def _L2_ffn_ref(x, router_weight, router_bias, w_gate, w_up, w_down):
        import jax, jax.numpy as jnp
        import numpy as np
        from jax import lax
        TOP_K = 4
        N_GROUP = 4
        TOPK_GROUP = 2
        ROUTED_SCALE = 2.5
        NEG_INF = -1000000000.0

        def _route(xf, router_weight, router_bias):
            T = xf.shape[0]
            E = router_weight.shape[0]
            logits = xf @ router_weight.T
            scores = jax.nn.sigmoid(logits)
            s_choice = scores + router_bias
            per_group = E // N_GROUP
            sg = s_choice.reshape(T, N_GROUP, per_group)
            group_scores = lax.top_k(sg, 2)[0].sum(-1)
            _, gidx = lax.top_k(group_scores, TOPK_GROUP)
            gmask = jnp.zeros((T, N_GROUP), dtype=bool).at[jnp.arange(T)[:, None], gidx].set(True)
            masked = jnp.where(gmask[:, :, None], sg, NEG_INF).reshape(T, E)
            _, topk_idx = lax.top_k(masked, TOP_K)
            w = jnp.take_along_axis(scores, topk_idx, axis=1)
            w = w / (w.sum(-1, keepdims=True) + 1e-20) * ROUTED_SCALE
            combine = jnp.zeros((T, E), dtype=xf.dtype).at[jnp.arange(T)[:, None], topk_idx].add(w)
            return combine
        B, S, H = x.shape
        E = w_gate.shape[0]
        xf = x.reshape(-1, H)
        combine = _route(xf, router_weight, router_bias)
        out = jnp.zeros_like(xf)
        for e in range(E):
            g = xf @ w_gate[e].T
            u = xf @ w_up[e].T
            y_e = jax.nn.silu(g) * u @ w_down[e].T
            out = out + combine[:, e:e + 1] * y_e
        return out.reshape(B, S, H)

    def _L3_attn_ref(x, Wq, Wk, Wv):
        import jax, jax.numpy as jnp
        import numpy as np
        GAMMA = 0.96875
        B, T, _ = x.shape
        D = Wq.shape[1]
        Q = jnp.einsum('bti,id->btd', x, Wq)
        K = jnp.einsum('bti,id->btd', x, Wk)
        V = jnp.einsum('bti,id->btd', x, Wv)
        gamma = jnp.asarray(GAMMA, x.dtype)
        m = jnp.einsum('btd,bt->td', K, V.sum(axis=-1))

        def step(s, mt):
            s_new = gamma * s + mt
            return (s_new, s_new)
        _, states = jax.lax.scan(step, jnp.zeros((D,), x.dtype), m[1:])
        S = jnp.concatenate([states[:1], states], axis=0)
        S = S.reshape(-1, T).T
        return S[None, :, :] * Q

    def _L3_ffn_ref(x, W1, b1, W2, b2):
        import jax, jax.numpy as jnp
        import numpy as np
        EMB = 128
        FF = 4 * EMB

        def _ternary(w):
            scale = jnp.maximum(jnp.mean(jnp.abs(w)), 1e-08)
            w_t = jnp.clip(jnp.round(w / scale), -1.0, 1.0)
            return w + jax.lax.stop_gradient(w_t - w)
        h = jnp.einsum('bsd,fd->bsf', x, _ternary(W1)) + b1
        h = jax.nn.gelu(h, approximate=False)
        out = jnp.einsum('bsf,df->bsd', h, _ternary(W2)) + b2
        return out
    x = L0_attn_inputs
    x = x + 0.5 * _L0_ffn_ref(_layernorm(x, axis=-1), L0_ffn_router_w, L0_ffn_w1, L0_ffn_b1, L0_ffn_w2, L0_ffn_b2)
    x = x + _L0_attn_ref(_layernorm(x, axis=-1), L0_attn_key_param_tokens, L0_attn_value_param_tokens)
    x = x + 0.5 * _L0_ffn_ref(_layernorm(x, axis=-1), L0_ffn_router_w, L0_ffn_w1, L0_ffn_b1, L0_ffn_w2, L0_ffn_b2)
    x = x + 0.5 * _L1_ffn_ref(_layernorm(x, axis=-1), L1_ffn_Wr, L1_ffn_br, L1_ffn_Wg, L1_ffn_bg, L1_ffn_W1, L1_ffn_b1, L1_ffn_W2, L1_ffn_b2, L1_ffn_D1, L1_ffn_d1b, L1_ffn_D2, L1_ffn_d2b)
    x = x + _L1_attn_ref(_layernorm(x, axis=-1), L1_attn_Wq, L1_attn_bq, L1_attn_Wk, L1_attn_bk, L1_attn_Wv, L1_attn_bv, L1_attn_Wo, L1_attn_bo)
    x = x + 0.5 * _L1_ffn_ref(_layernorm(x, axis=-1), L1_ffn_Wr, L1_ffn_br, L1_ffn_Wg, L1_ffn_bg, L1_ffn_W1, L1_ffn_b1, L1_ffn_W2, L1_ffn_b2, L1_ffn_D1, L1_ffn_d1b, L1_ffn_D2, L1_ffn_d2b)
    x = x + 0.5 * _L2_ffn_ref(_layernorm(x, axis=-1), L2_ffn_router_weight, L2_ffn_router_bias, L2_ffn_w_gate, L2_ffn_w_up, L2_ffn_w_down)
    x = x + _L2_attn_ref(_layernorm(x, axis=-1), L2_attn_Wq, L2_attn_Wk, L2_attn_Wv, L2_attn_Wo)
    x = x + 0.5 * _L2_ffn_ref(_layernorm(x, axis=-1), L2_ffn_router_weight, L2_ffn_router_bias, L2_ffn_w_gate, L2_ffn_w_up, L2_ffn_w_down)
    x = x + 0.5 * _L3_ffn_ref(_layernorm(x, axis=-1), L3_ffn_W1, L3_ffn_b1, L3_ffn_W2, L3_ffn_b2)
    x = x + _L3_attn_ref(_layernorm(x, axis=-1), L3_attn_Wq, L3_attn_Wk, L3_attn_Wv)
    x = x + 0.5 * _L3_ffn_ref(_layernorm(x, axis=-1), L3_ffn_W1, L3_ffn_b1, L3_ffn_W2, L3_ffn_b2)
    return x

_drawn_inputs = setup_inputs


def setup_inputs(seed=0):
    import zlib

    import numpy as np

    out = dict(_drawn_inputs(seed))
    spreads = {'L0_ffn_b1': (0.0, 0.1),
     'L0_ffn_b2': (0.0, 0.1),
     'L1_attn_bq': (0.0, 0.322),
     'L1_attn_bk': (0.0, 2.0),
     'L1_attn_bv': (0.0, 0.1),
     'L1_attn_bo': (0.0, 0.1),
     'L1_ffn_br': (0.0, 0.8),
     'L1_ffn_bg': (0.0, 0.1),
     'L1_ffn_b1': (0.0, 0.1),
     'L1_ffn_b2': (0.0, 0.1),
     'L1_ffn_d1b': (0.0, 0.1),
     'L1_ffn_d2b': (0.0, 0.1),
     'L2_ffn_router_bias': (0.0, 0.8)}
    factors = {'L2_ffn_router_weight': 8.0,
     'L2_ffn_w_gate': 8.0,
     'L2_ffn_w_up': 8.0,
     'L2_ffn_w_down': 8.0,
     'L3_ffn_b1': 7.036,
     'L3_ffn_b2': 26.324}
    for name, (base, spread) in spreads.items():
        noise = np.random.default_rng([zlib.crc32(name.encode()), seed]).standard_normal(out[name].shape)
        drawn = base * np.exp(spread * noise) if base else spread * noise
        out[name] = jnp.asarray(drawn.astype(out[name].dtype))
    for name, factor in factors.items():
        out[name] = (out[name] * factor).astype(out[name].dtype)
    return out
```

```python
from contextlib import ExitStack

import numpy as np

import concourse.bass as bass
from concourse import mybir

F32 = mybir.dt.float32
F32R = mybir.dt.float32r
U32 = mybir.dt.uint32
BF16 = mybir.dt.bfloat16
ALU = mybir.AluOpType
ACT = mybir.ActivationFunctionType
AX = mybir.AxisListType

P = 128
D = 128
B, T = 16, 256
TOK = B * T
CH = 512
NT = CH // P
NC = TOK // CH
SEQ = CH // T
LN_EPS = 1e-5
NEG = -1e9
LOWEST = -3.0e38
HEADS = 16
HD = D // HEADS
GAMMA = 0.96875

FF0 = dict(kind="ffn", name="ff0", n=16, ne=8, act=ACT.Gelu, route="softmax", coef=0.5)
PAT = dict(kind="pattention", name="pat", n=4, ne=1, act=ACT.Gelu, route=None, coef=1.0)
FF1 = dict(kind="ffn", name="ff1", n=36, ne=9, act=ACT.Relu, route="softmax_dense", coef=0.5)
AT1 = dict(kind="attention", name="at1", n=0, ne=0, act=None, route=None, coef=1.0, heads=16, per=2)
GLU = dict(kind="glu", name="glu", n=8, ne=8, act=ACT.Silu, route="grouped", coef=0.5)
AT2 = dict(kind="attention", name="at2", n=0, ne=0, act=None, route=None, coef=1.0, heads=1, per=1)
FF3 = dict(kind="ffn", name="ff3", n=4, ne=1, act=ACT.Gelu, route=None, coef=0.5)
RET = dict(kind="retention", name="ret", n=0, ne=0, act=None, route=None, coef=1.0)
LAYERS = [FF0, PAT, FF0, FF1, AT1, FF1, GLU, AT2, GLU, FF3, RET, FF3]

def columns(parts):
    at, out = 0, {}
    for name, width in parts:
        out[name] = (at, width)
        at += width
    return out, at


W0_COLS, W0_N = columns([(f"{w}{e}", 256) for e in range(8) for w in ("w1_", "w2_")])
WS_COLS, WS_N = columns([("router0", D), ("router1", D), ("key", 512), ("value", 512),
                         ("wq1", D), ("wk1", D), ("wv1", D), ("wo1", D)])
WB_COLS, WB_N = columns([("w1", 36 * D), ("w2", 36 * D)])
WA_COLS, WA_N = columns([("gate", 8 * D), ("up", 8 * D), ("down", 8 * D), ("router2", D), ("sel2", 8 * D),
                         ("wq2", D), ("wk2", D), ("wv2", D), ("wo2", D),
                         ("wq3", D), ("wk3", D), ("wv3", D), ("pad", D)])
W3_N = 8 * D
B_PIECE = WB_N // (3 * NC)
A_PIECE = WA_N // NC
assert B_PIECE * 3 * NC == WB_N and A_PIECE * NC == WA_N
C_COLS, C_N = columns([("ident", P), ("iota", 16), ("bias2", 16), ("b1_0", 16), ("b2_0", 8),
                       ("b1_1", 36), ("b2_1", 9), ("b1_3", 4), ("b2_3", 1), ("rb0", 1), ("rb1", 1), ("rb2", 1),
                       ("bq", 1), ("bk", 1), ("bo", 1), ("bv", D), ("hmask", HEADS), ("cmask", P)])

HOOKS = ["fin", "stats", "z", "zT", "zsplit", "logits", "logitsT", "back", "r1", "rx", "r2", "cs", "cT"]
R_STEPS = {"softmax": 13, "softmax_dense": 14, "grouped": 23}
TERNARY_STEPS = 14
R_BEFORE_EXP = {"softmax": 3, "softmax_dense": 3, "grouped": 1}
R_WIDTH = {"softmax": 8, "softmax_dense": 10, "grouped": 16}
FIRST = [("ws", 0, 256)] + [("w0", i * 512, 512) for i in range(8)] + [("ws", 256 + i * 512, 512) for i in range(3)]


def twelve_sublayers(nc, x_in, w0, ws, wb, wa, w3, cst, sel, x_out, layers=LAYERS):
    NL = len(layers)
    with ExitStack() as ctx:
        def sb(name, shape, dt=F32):
            return ctx.enter_context(nc.sbuf_tensor(name, shape, dt))

        def sem(name):
            return ctx.enter_context(nc.semaphore(name))

        x = sb("x", [P, TOK])
        z_hi, z_lo = sb("z_hi", [P, 2, CH], F32R), sb("z_lo", [P, 2, CH], F32R)
        ws_hi, ws_lo = sb("ws_hi", [P, WS_N], F32R), sb("ws_lo", [P, WS_N], F32R)
        with nc.sbuf_tensor("values2", [P, NT, D], F32) as values2, nc.sbuf_tensor("turned_p2", [P, 2, 6 * P], F32) as turned_p2, \
                nc.sbuf_tensor("queries", [P, TOK], F32) as queries, nc.sbuf_tensor("moments", [P, 2, T], F32) as moments, \
                nc.sbuf_tensor("decay", [P, T], F32) as decay, nc.sbuf_tensor("states", [P, T], F32) as states, \
                nc.sbuf_tensor("states_t", [P, T], F32) as states_t, nc.sbuf_tensor("ternary", [P, 4, 512], F32) as ternary, \
                nc.sbuf_tensor("w3_hi", [P, W3_N], F32R) as w3_hi, nc.sbuf_tensor("w3_lo", [P, W3_N], F32R) as w3_lo:
            pass
        wb_hi, wb_lo = sb("wb_hi", [P, WB_N], F32R), sb("wb_lo", [P, WB_N], F32R)
        with nc.sbuf_tensor("w0_hi", [P, W0_N], F32R) as w0_hi, nc.sbuf_tensor("w0_lo", [P, W0_N], F32R) as w0_lo:
            pass
        with nc.sbuf_tensor("values1", [P, NT, HEADS * (D + HD)], F32) as values1, nc.sbuf_tensor("turned_p1", [P, 2, 6 * P], F32) as turned_p1:
            pass
        wa_hi, wa_lo = sb("wa_hi", [P, WA_N], F32R), sb("wa_lo", [P, WA_N], F32R)
        sel1 = sb("sel1", [32, 9, P], F32R)
        stage = sb("stage", [P, 2, A_PIECE])
        consts = sb("consts", [P, C_N])
        hidden = sb("hidden", [P, 3, CH])
        h_hi, h_lo = sb("h_hi", [P, 3, CH], F32R), sb("h_lo", [P, 3, CH], F32R)
        gain = sb("gain", [P, 2, CH])
        scaled = sb("scaled", [P, 2, CH])
        yT = sb("yT", [P, CH])
        z_tok = sb("z_tok", [P, NT, D])
        stats = sb("stats", [P, NT, 6])
        mean_var = sb("mean_var", [P, NT, 2])
        var_eps = sb("var_eps", [P, NT])
        rstd = sb("rstd", [P, NT])
        minus_half = sb("minus_half", [P, NT])
        eps, per_key = sb("eps", [P, NT]), sb("per_key", [P, NT])
        lgT = sb("lgT", [P, CH])
        lg = sb("lg", [P, NT, 16])
        ex = sb("ex", [P, NT, 16])
        top8 = sb("top8", [P, NT, 8])
        at8 = sb("at8", [P, NT, 8], U32)
        at8f = sb("at8f", [P, NT, 8])
        mask = sb("mask", [P, NT, 16])
        hit = sb("hit", [P, NT, 16, 4])
        r_sum = sb("r_sum", [P, NT, 2])
        cw = sb("cw", [P, NT, 16])
        cs = sb("cs", [P, NT, 32])
        cs_r = sb("cs_r", [P, NT, 16], F32R)
        groups = sb("groups", [P, NT, 8])
        gmask = sb("gmask", [P, NT, 4])
        gfill = sb("gfill", [P, NT, 4])
        masked = sb("masked", [P, NT, 16])
        pair6 = sb("pair6", [P, NT, 4, 6])
        cT = sb("cT", [32, 2, CH], F32R)
        norm = sb("norm", [P, NT])
        row_max = sb("row_max", [P, 2, 4])
        neg_max = sb("neg_max", [P, 2, 4])
        row_sum = sb("row_sum", [P, NT, HEADS])
        inv_sum = sb("inv_sum", [P, NT, HEADS])
        ones_r = sb("ones_r", [P, P], F32R)
        ones = sb("ones", [P, P])
        waited = sb("waited", [P, 1])
        ident_b, cmask_b = sb("ident_b", [P, P], BF16), sb("cmask_b", [P, P], BF16)
        w_size = sb("w_size", [P, 8])

        def const(name, rows=P, lo=0, hi=None):
            a, w = C_COLS[name]
            return consts[0:rows, a + lo:a + (w if hi is None else hi)]

        ident = const("ident")

        bank = [ctx.enter_context(nc.psum_tensor(f"bank{i}", [P, CH], F32)) for i in range(8)]
        h_bank = [bank[0], bank[1], bank[4]]
        y_bank = [bank[2], bank[3]]
        gain_bank = bank[5]
        turn_bank = bank[6]
        route_bank = bank[7]

        first_in, consts_in, rest_in = sem("first_in"), sem("consts_in"), sem("rest_in")
        first_piece_in = [sem("first_piece_in0"), sem("first_piece_in1")]
        first_piece_hi, first_piece_split = sem("first_piece_hi"), sem("first_piece_split")
        piece_in = [sem("piece_in0"), sem("piece_in1")]
        piece_hi, piece_split = sem("piece_hi"), sem("piece_split")
        sel_in, sel_ready = sem("sel_in"), sem("sel_ready")
        x_stored = sem("x_stored")
        const_ready = sem("const_ready")
        stats_done, mean_done, eps_added, rstd_done = sem("stats_done"), sem("mean_done"), sem("eps_added"), sem("rstd_done")
        z_done, zT_done, zhi_done, zlo_done = sem("z_done"), sem("zT_done"), sem("zhi_done"), sem("zlo_done")
        logits_done, lgT_done, back_done = sem("logits_done"), sem("lgT_done"), sem("back_done")
        route_step, exp_done, csT_done, cT_done = sem("route_step"), sem("exp_done"), sem("csT_done"), sem("cT_done")
        up_done, act_done = sem("up_done"), sem("act_done")
        hi_by_act, hi_by_dve, lo_done = sem("hi_by_act"), sem("hi_by_dve"), sem("lo_done")
        gain_mm, gain_done = sem("gain_mm"), sem("gain_done")
        y_done, scaled_done = sem("y_done"), sem("scaled_done")
        added = sem("added")
        yT_done, turned, x_done = sem("yT_done"), sem("turned"), sem("x_done")
        pa_logits, pa_squares, pa_mean, pa_norm, pa_gelu = sem("pa_logits"), sem("pa_squares"), sem("pa_mean"), sem("pa_norm"), sem("pa_gelu")
        pa_turned, pa_hi, pa_lo, pa_y = sem("pa_turned"), sem("pa_hi"), sem("pa_lo"), sem("pa_y")
        at_proj, at_qk, at_v, at_keys = sem("at_proj"), sem("at_qk"), sem("at_v"), sem("at_keys")
        at_scores, at_max, at_negmax, at_probs = sem("at_scores"), sem("at_max"), sem("at_negmax"), sem("at_probs")
        at_turned, at_out_a, at_out_d, at_pv = sem("at_turned"), sem("at_out_a"), sem("at_out_d"), sem("at_pv")
        at_raw, at_tok, at_inv, at_norm, at_back, at_hi, at_lo, at_y = [sem(n) for n in (
            "at_raw", "at_tok", "at_inv", "at_norm", "at_back", "at_hi", "at_lo", "at_y")]
        glu_mm, silu_done, glu_uv, glu_h, glu_hi, glu_lo, glu_y = [sem(n) for n in (
            "glu_mm", "silu_done", "glu_uv", "glu_h", "glu_hi", "glu_lo", "glu_y")]
        zeroed = sem("zeroed")
        setup_done = sem("setup_done")
        ternary_sum, ternary_total, ternary_step = sem("ternary_sum"), sem("ternary_total"), sem("ternary_step")
        rt_proj, rt_keys, rt_vhi, rt_queries, rt_vlo, rt_vsum, rt_kv, rt_moment = [sem(n) for n in (
            "rt_proj", "rt_keys", "rt_vhi", "rt_queries", "rt_vlo", "rt_vsum", "rt_kv", "rt_moment")]
        rt_scan, rt_states, rt_states_t, rt_ready = sem("rt_scan"), sem("rt_states"), sem("rt_states_t"), sem("rt_ready")

        def wait(eng, s, value):
            if isinstance(value, int) and value <= 0:
                return
            eng.wait_ge(s, value)

        def before(L, f):
            return sum(f(layers[i]) for i in range(L)) * NC

        TILES = [before(L, lambda y: y["n"] if y["kind"] in ("ffn",) else 0) for L in range(NL + 1)]
        ROUTED = [before(L, lambda y: 1 if y["route"] else 0) for L in range(NL + 1)]
        EXPERTS = [before(L, lambda y: y["ne"] if y["kind"] in ("ffn",) else 0) for L in range(NL + 1)]
        GAINS = [before(L, lambda y: y["ne"] if y["route"] else 0) for L in range(NL + 1)]
        ADDS = [before(L, lambda y: y["ne"] - 1 if y["kind"] == "ffn" and y["route"] else 0) for L in range(NL + 1)]
        PAIRS = [before(L, lambda y: y["n"] if y["kind"] == "glu" else 0) for L in range(NL + 1)]
        GLUS = [before(L, lambda y: 1 if y["kind"] == "glu" else 0) for L in range(NL + 1)]
        PATS = [before(L, lambda y: 1 if y["kind"] == "pattention" else 0) for L in range(NL + 1)]
        ATTS = [before(L, lambda y: 1 if y["kind"] == "attention" else 0) for L in range(NL + 1)]
        GROUPS = [before(L, lambda y: SEQ * y["heads"] // y["per"] if y["kind"] == "attention" else 0) for L in range(NL + 1)]
        RSTEPS = [before(L, lambda y: R_STEPS[y["route"]] if y["route"] else 0) for L in range(NL + 1)]

        class Job:

            def __init__(self, L, c, u, pair=0):
                self.L, self.c, self.u, self.pair, self.y = L, c, u, pair, layers[L]
                self.J = L * NC + c
                self.R = ROUTED[L] + c
                n, ne = self.y["n"], self.y["ne"]
                self.tiles = TILES[L] + c * n
                self.half_tiles = TILES[L] // 2 + c * (n // 2)
                self.experts = EXPERTS[L] + c * ne
                self.gains = GAINS[L] + c * ne
                self.adds = ADDS[L] + c * (ne - 1)
                self.rsteps = RSTEPS[L] + c * R_STEPS.get(self.y["route"], 0)

        def job_first(job):
            return isinstance(job.c, int) and job.c == 0

        def job_is_last(job):
            return job.L == NL - 1 and isinstance(job.c, int) and job.c == NC - 1

        YT = [before(L, lambda y: 0 if y["kind"] == "ffn" and y["route"] else 1) for L in range(NL + 1)]

        def each_job(eng, main):
            for L in range(NL):
                def pair(c0, number):
                    for u in range(2):
                        c = c0 + u
                        job = Job(L, c, u, number)
                        if u == 1:
                            prev = Job(L, c0, 0)
                        elif isinstance(c0, int) and c0 == 0:
                            prev = Job(L - 1, NC - 1, 1) if L else None
                        else:
                            prev = Job(L, c0 - 1, 1)
                        if prev is not None and prev.y["kind"] == "retention":
                            prev = None
                        if isinstance(c, int) and c == NC - 1:
                            after = Job(L + 1, 0, 0) if L + 1 < NL else None
                        else:
                            after = Job(L, c + 1, 1 - u)
                        main(job, prev, after)
                pair(0, 0)
                with eng.Fori(1, NC // 2 - 1) as i:
                    pair(i * 2, i)
                pair(NC - 2, NC // 2 - 1)

        def hook_names(after):
            names = list(HOOKS) if after is not None else ["fin"]
            return names if after is None or after.y["route"] else names[:5]

        def spread(names, points):
            out = [[] for _ in range(points)]
            for i, h in enumerate(names):
                out[min(points - 1, i * points // len(names))].append(h)
            return out

        def attention_hooks(job, after):
            groups = SEQ * job.y["heads"] // job.y["per"]
            names = hook_names(after)
            return spread(names[:5], groups), names[5:]

        def hooks_at(job, after):
            names = hook_names(after)
            n = job.y["n"]
            out = [[] for _ in range(n)]
            for i, h in enumerate(names):
                out[min(n - 1, 1 + i * (n - 1) // len(names))].append(h)
            return out

        def weights(job, part, k):
            name = job.y["name"]
            if name == "ff0":
                a = W0_COLS[f"{part}_{k // 2}"][0] + (k % 2) * P
                return w0_hi[:, a:a + P], w0_lo[:, a:a + P]
            if name == "ff3":
                a = (0 if part == "w1" else 512) + k * P
                return w3_hi[:, a:a + P], w3_lo[:, a:a + P]
            if name == "ff1":
                a = WB_COLS[part][0] + k * P
                return wb_hi[:, a:a + P], wb_lo[:, a:a + P]
            raise ValueError(name)

        def small(name, lo=0, hi=None):
            a, w = WS_COLS[name]
            s = slice(a + lo, a + (w if hi is None else hi))
            return ws_hi[:, s], ws_lo[:, s]

        def late(name, lo=0, hi=None):
            a, w = WA_COLS[name]
            s = slice(a + lo, a + (w if hi is None else hi))
            return wa_hi[:, s], wa_lo[:, s]

        def router(job):
            return {"ff0": lambda: small("router0"), "ff1": lambda: small("router1"),
                    "glu": lambda: late("router2")}[job.y["name"]]()


        def pat_rows(t):
            return hidden[:, t, :] if t < 3 else gain[:, 0, :]

        def glu_bank(which, k):
            return bank[2 * (k % 2) + which]

        def attention_buffers(job):
            return (values1, turned_p1) if job.y["heads"] > 1 else (values2, turned_p2)

        block = ctx.enter_context(nc.Block())

        @block.sync
        def _(sp):
            xv = x[:, :].rearrange("p (t d) -> p t d", d=D)
            xd = x_in.rearrange("b (t p) d -> p (b t) d", p=P)
            od = x_out.rearrange("b (t p) d -> p (b t) d", p=P)
            sp.dma_start(xv[:, 0:NT, :], xd[:, 0:NT, :]).then_inc(first_in, 16)
            sp.dma_start(consts[:, :], cst).then_inc(consts_in, 16)
            sp.dma_start(hidden[0:32, :, :].rearrange("p a n -> p (a n)")[:, 0:9 * P], sel).then_inc(sel_in, 16)
            for i, (src, at, n) in enumerate(FIRST):
                if i >= 2:
                    sp.wait_ge(first_piece_split, i - 1)
                sp.dma_start(stage[:, i % 2, 0:n], {"ws": ws, "w0": w0}[src][:, at:at + n]).then_inc(first_piece_in[i % 2], 16)
                if i == 1:
                    sp.dma_start(xv[:, NT:, :], xd[:, NT:, :]).then_inc(rest_in, 16)
            if NL > 3:
                sp.wait_ge(first_piece_split, len(FIRST))
                for n in range(2):
                    sp.dma_start(stage[:, n, 0:B_PIECE], wb[:, n * B_PIECE:(n + 1) * B_PIECE]).then_inc(piece_in[n], 16)
                with sp.Fori(1, 3 * NC // 2) as i:
                    for u in range(2):
                        sp.wait_ge(piece_split, i * 2 + (u - 1))
                        sp.dma_start(stage[:, u, 0:B_PIECE],
                                     wb[:, bass.ds(i * (2 * B_PIECE) + u * B_PIECE, B_PIECE)]).then_inc(piece_in[u], 16)
            if NL > 6:
                for n in range(NC):
                    sp.wait_ge(piece_split, 3 * NC + n - 1)
                    sp.dma_start(stage[:, n % 2, 0:A_PIECE], wa[:, n * A_PIECE:(n + 1) * A_PIECE]).then_inc(piece_in[n % 2], 16)
                for n in range(2):
                    sp.wait_ge(piece_split, 4 * NC + n - 1)
                    sp.dma_start(stage[:, n, 0:512], w3[:, n * 512:(n + 1) * 512]).then_inc(piece_in[n], 16)
            sp.wait_ge(x_done, NL * NC)
            sp.dma_start(od, xv).then_inc(x_stored, 16)
            sp.wait_ge(x_stored, 16)

        @block.gpsimd
        def _(pool):
            nc.gpsimd.memset(minus_half[:, :], -0.5)
            nc.gpsimd.memset(eps[:, :], LN_EPS)
            nc.gpsimd.memset(per_key[:, :], 1.0 / 512)
            nc.gpsimd.memset(ones[:, :], 1.0)
            nc.gpsimd.memset(cw[:, :, :], 0.0)
            nc.gpsimd.memset(lgT[:, :], 0.0)
            nc.gpsimd.memset(groups[:, :, :], LOWEST).then_inc(const_ready, 1)
            pool.wait_ge(const_ready, 1)

            def rstd_of(job):
                pool.wait_ge(mean_done, job.J + 1)
                nc.gpsimd.tensor_tensor(var_eps[:, :], mean_var[:, :, 1], eps[:, :], ALU.add).then_inc(eps_added, 1)
                pool.wait_ge(eps_added, job.J + 1)
                wait(pool, z_done, job.J)
                nc.gpsimd.tensor_tensor(rstd[:, :], var_eps[:, :], minus_half[:, :], ALU.pow).then_inc(rstd_done, 1)

            def split_piece(number, slot, of_slot, hi, lo, n):
                w = stage[:, slot, 0:n]
                pool.wait_ge(piece_in[slot], of_slot * 16)
                nc.gpsimd.tensor_copy(hi, w).then_inc(piece_hi, 1)
                pool.wait_ge(piece_hi, number + 1)
                nc.gpsimd.tensor_tensor(lo, w, hi.bitcast(F32), ALU.subtract).then_inc(piece_split, 1)

            def weights_ahead(job):
                if job.L < 3 and NL > 3:
                    at = bass.ds(job.J * B_PIECE, B_PIECE)
                    split_piece(job.J, job.u, (job.L * NC // 2) + job.pair + 1, wb_hi[:, at], wb_lo[:, at], B_PIECE)
                if job.L == 5 and NL > 6:
                    at = bass.ds(job.c * A_PIECE, A_PIECE)
                    split_piece(job.c + 3 * NC, job.u, (3 * NC // 2) + job.pair + 1, wa_hi[:, at], wa_lo[:, at], A_PIECE)

            def add_expert(job, e):
                pool.wait_ge(scaled_done, job.gains + e + 1)
                if e == 1:
                    wait(pool, turned, job.J)
                    a = scaled[:, 0, :]
                else:
                    pool.wait_ge(added, job.adds + e - 1)
                    a = yT[:, :]
                nc.gpsimd.tensor_tensor(yT[:, :], a, scaled[:, e % 2, :], ALU.add).then_inc(added, 1)

            def main(job, prev, after):
                y = job.y
                if y["kind"] == "ffn":
                    per = y["n"] // y["ne"]
                    for k in range(y["n"] + 2):
                        if k < y["n"] and "stats" in hooks_at(job, after)[k]:
                            rstd_of(after)
                        if y["route"] and (k - 2) % per == per - 1 and k - 2 >= per:
                            add_expert(job, (k - 2) // per)
                        if k == 3:
                            weights_ahead(job)
                elif y["kind"] == "pattention":
                    pool.wait_ge(pa_squares, (PATS[job.L] + job.c) * NT + NT)
                    nc.gpsimd.tensor_tensor(norm[:, :], norm[:, :], per_key[:, :], ALU.mult).then_inc(pa_mean, 1)
                    pool.wait_ge(pa_mean, PATS[job.L] + job.c + 1)
                    nc.gpsimd.tensor_tensor(norm[:, :], norm[:, :], minus_half[:, :], ALU.pow).then_inc(pa_norm, 1)
                    if after is not None:
                        rstd_of(after)
                    weights_ahead(job)
                elif y["kind"] == "attention":
                    keys_of_heads(job, after)
                elif y["kind"] == "retention":
                    if after is not None:
                        rstd_of(after)
                elif y["kind"] == "glu":
                    hooks = hooks_at(job, after)
                    for k in range(y["n"]):
                        pool.wait_ge(glu_uv, PAIRS[job.L] + job.c * y["n"] + k + 1)
                        pool.wait_ge(gain_done, job.gains + k + 1)
                        wait(pool, glu_lo, PAIRS[job.L] + job.c * y["n"] + (k - 2 if k >= 3 else 0))
                        nc.gpsimd.tensor_tensor(hidden[:, k % 3, :], scaled[:, k % 2, :], gain[:, k % 2, :], ALU.mult).then_inc(glu_h, 1)
                        if k >= 1 and "stats" in hooks[k - 1]:
                            rstd_of(after)

            def keys_of_heads(job, after):
                y = job.y
                groups = SEQ * y["heads"] // y["per"]
                hooks, late_hooks = attention_hooks(job, after)
                G = GROUPS[job.L] + job.c * groups
                if y["heads"] > 1 and isinstance(job.c, int) and job.c == 0:
                    pool.wait_ge(x_done, job.L * NC - 1)
                    nc.gpsimd.memset(values1[:, :, :], 0.0).then_inc(zeroed, 1)
                for g in range(groups):
                    if y["heads"] > 1:
                        b, hp = g // (groups // SEQ), g % (groups // SEQ)
                        if g == 0:
                            pool.wait_ge(at_qk, (ATTS[job.L] + job.c) * 2 + 2)
                        wait(pool, at_scores, G + g - 1)
                        pool_k = scaled[:, 1, b * T:(b + 1) * T].rearrange("p (o t) -> p o t", o=1).broadcast_to([P, 2, T])
                        hm = const("hmask", P, 2 * hp, 2 * hp + 2).rearrange("p (h o) -> p h o", o=1).broadcast_to([P, 2, T])
                        nc.gpsimd.tensor_tensor(gain[:, g % 2, :].rearrange("p (h t) -> p h t", h=2), pool_k, hm,
                                                ALU.mult).then_inc(at_keys, 1)
                    if "stats" in hooks[g]:
                        rstd_of(after)

            rstd_of(Job(0, 0, 0))
            each_job(pool, main)

        @block.scalar
        def _(act):
            def hook(h, after):
                if h == "zsplit":
                    act.wait_ge(zT_done, after.J + 1)
                    nc.scalar.activation(z_hi[:, after.u, :], turn_bank[:, :], ACT.Copy).then_inc(zhi_done, 1)
                elif h == "logitsT":
                    act.wait_ge(logits_done, after.R + 1)
                    bias = {"ff0": "rb0", "ff1": "rb1", "glu": "rb2"}[after.y["name"]]
                    nc.scalar.activation(lgT[0:32, :], route_bank[0:32, :], ACT.Identity,
                                         bias=const(bias, 32)).then_inc(lgT_done, 1)
                elif h == "rx":
                    route = after.y["route"]
                    w = R_WIDTH[route]
                    act.wait_ge(route_step, after.rsteps + R_BEFORE_EXP[route])
                    src = lg if route == "grouped" else masked
                    nc.scalar.activation(ex[:, :, 0:w], src[:, :, 0:w],
                                         ACT.Sigmoid if route == "grouped" else ACT.Exp).then_inc(exp_done, 1)
                elif h == "cT":
                    act.wait_ge(csT_done, after.R + 1)
                    nc.scalar.activation(cT[:, after.u, :], route_bank[0:32, :], ACT.Copy).then_inc(cT_done, 1)

            def tile(job, k):
                y = job.y
                act.wait_ge(up_done, job.tiles + k + 1)
                wait(act, lo_done, job.tiles + (k - 2 if k >= 3 else 0))
                bias = const({"ff0": "b1_0", "ff1": "b1_1", "ff3": "b1_3"}[y["name"]], P, k, k + 1)
                nc.scalar.activation(hidden[:, k % 3, :], h_bank[k % 3][:, :], y["act"], bias=bias).then_inc(act_done, 1)
                if k % 2 == 0:
                    act.wait_ge(act_done, job.tiles + k + 1)
                    nc.scalar.activation(h_hi[:, k % 3, :], hidden[:, k % 3, :], ACT.Copy).then_inc(hi_by_act, 1)

            def gain_of(job, e):
                act.wait_ge(gain_mm, job.gains + e + 1)
                wait(act, scaled_done, job.gains + (e - 1 if e >= 2 else 0))
                nc.scalar.activation(gain[:, e % 2, :], gain_bank[:, :], ACT.Copy).then_inc(gain_done, 1)

            def main(job, prev, after):
                y = job.y
                if y["kind"] == "ffn":
                    per = y["n"] // y["ne"]
                    hooks = hooks_at(job, after)
                    for k in range(y["n"]):
                        tile(job, k)
                        if y["route"] and k % per == 1:
                            gain_of(job, k // per)
                        for h in hooks[k]:
                            hook(h, after)
                elif y["kind"] == "pattention":
                    n0 = PATS[job.L] + job.c
                    hooks = spread(hook_names(after), 6)
                    for h in hooks[0]:
                        hook(h, after)
                    for t in range(NT):
                        act.wait_ge(pa_logits, n0 * NT + t + 1)
                        if t == 0:
                            wait(act, pa_norm, n0)
                            wait(act, pa_turned, n0 * NT)
                            wait(act, pa_gelu, n0 * NT)
                        nc.scalar.activation(pat_rows(t), bank[t][:, :], ACT.Square,
                                             accum_out=norm[:, t:t + 1]).then_inc(pa_squares, 1)
                    for h in hooks[1]:
                        hook(h, after)
                    act.wait_ge(pa_norm, n0 + 1)
                    for t in range(NT):
                        nc.scalar.activation(pat_rows(t), bank[t][:, :], ACT.Gelu, scale=norm[:, t:t + 1]).then_inc(pa_gelu, 1)
                    for k in range(4):
                        act.wait_ge(pa_turned, n0 * NT + k + 1)
                        nc.scalar.activation(h_hi[:, k % 3, :], bank[4 + k % 2][:, :], ACT.Copy).then_inc(pa_hi, 1)
                        for h in hooks[2 + k]:
                            hook(h, after)
                elif y["kind"] == "attention":
                    if y["heads"] == 1 and isinstance(job.c, int) and job.c == 0:
                        for m in range(2):
                            act.wait_ge(piece_in[m], 16 * (3 * NC // 2 + NC // 2 + 1))
                            nc.scalar.activation(ternary[:, m, :], stage[:, m, 0:512], ACT.Abs,
                                                 accum_out=w_size[:, m:m + 1]).then_inc(ternary_sum, 1)
                    attention(job, after)
                elif y["kind"] == "retention":
                    if job_first(job):
                        act.wait_ge(yT_done, YT[job.L])
                    act.wait_ge(rt_proj, job.c * 3 + 1)
                    wait(act, rt_kv, job.c)
                    nc.scalar.activation(gain[:, 0, :], bank[0][:, :], ACT.Copy).then_inc(rt_keys, 1)
                    act.wait_ge(rt_proj, job.c * 3 + 2)
                    nc.scalar.activation(h_hi[:, 0, :], bank[1][:, :], ACT.Copy).then_inc(rt_vhi, 1)
                    act.wait_ge(rt_proj, job.c * 3 + 3)
                    nc.scalar.activation(queries[:, bass.ds(job.c * CH, CH)], bank[2][:, :], ACT.Copy).then_inc(rt_queries, 1)
                    for h in hook_names(after):
                        hook(h, after)
                elif y["kind"] == "glu":
                    n0 = PAIRS[job.L] + job.c * y["n"]
                    hooks = hooks_at(job, after)
                    for k in range(y["n"]):
                        act.wait_ge(glu_mm, n0 + k + 1)
                        if k < 2:
                            wait(act, glu_h, n0)
                        else:
                            act.wait_ge(glu_h, n0 + k - 1)
                        nc.scalar.activation(scaled[:, k % 2, :], glu_bank(0, k)[:, :], ACT.Silu).then_inc(silu_done, 1)
                        act.wait_ge(gain_mm, job.gains + k + 1)
                        nc.scalar.activation(gain[:, k % 2, :], gain_bank[:, :], ACT.Copy).then_inc(gain_done, 1)
                        if k >= 1:
                            glu_split(n0, k - 1)
                            for h in hooks[k - 1]:
                                hook(h, after)
                    glu_split(n0, y["n"] - 1)
                    for h in hooks[-1]:
                        hook(h, after)

            def glu_split(n0, k):
                act.wait_ge(glu_h, n0 + k + 1)
                nc.scalar.activation(h_hi[:, k % 3, :], hidden[:, k % 3, :], ACT.Copy).then_inc(glu_hi, 1)

            def attention(job, after):
                y = job.y
                heads, per = y["heads"], y["per"]
                groups = SEQ * heads // per
                A = ATTS[job.L] + job.c
                G = GROUPS[job.L] + job.c * groups
                hooks, late_hooks = attention_hooks(job, after)
                scale = float(D // heads) ** -0.5
                probs = hidden[:, :, :].rearrange("p a n -> p (a n)").rearrange("p (s n) -> p s n", s=2)
                _, turned_p = attention_buffers(job)
                for i, name in enumerate(("bq", "bk")):
                    act.wait_ge(at_proj, A * 3 + i + 1)
                    if i == 0:
                        wait(act, at_y, A)
                    if heads > 1:
                        nc.scalar.activation(scaled[:, i, :], bank[i][:, :], ACT.Identity, bias=const(name)).then_inc(at_qk, 1)
                    else:
                        nc.scalar.activation(scaled[:, i, :], bank[i][:, :], ACT.Copy).then_inc(at_qk, 1)

                def turned_out(g):
                    act.wait_ge(at_turned, G + g + 1)
                    wait(act, at_pv, G + g - 1)
                    nc.scalar.activation(turned_p[:, g % 2, 0:2 * per * P], bank[4][:, 0:2 * per * P], ACT.Copy).then_inc(at_out_a, 1)

                for g in range(groups):
                    b, hp = g // (groups // SEQ), g % (groups // SEQ)
                    act.wait_ge(at_negmax, G + g + 1)
                    wait(act, at_turned, G + g - 1)
                    if g == 0:
                        wait(act, at_back, A)
                        wait(act, at_norm, A)
                    for qb in range(2):
                        for h in range(per):
                            keys = (qb + 1) * P
                            at = h * P if qb == 0 else per * P + h * 2 * P
                            src = bank[2 * (g % 2) + qb][:, h * keys:(h + 1) * keys]
                            ins = nc.scalar.activation(probs[:, g % 2, at:at + keys], src, ACT.Exp,
                                                       bias=neg_max[:, g % 2, qb * per + h:qb * per + h + 1], scale=scale,
                                                       accum_out=row_sum[:, 2 * b + qb, hp * per + h:hp * per + h + 1])
                    ins.then_inc(at_probs, 1)
                    if g >= 1:
                        turned_out(g - 1)
                    for h in hooks[g]:
                        hook(h, after)
                turned_out(groups - 1)
                act.wait_ge(at_pv, G + groups)
                wait(act, turned, job.J)
                nc.scalar.activation(yT[:, :], bank[7][:, :], ACT.Copy).then_inc(at_raw, 1)
                act.wait_ge(at_back, A + 1)
                nc.scalar.activation(h_hi[:, 0, :], bank[5][:, :], ACT.Copy).then_inc(at_hi, 1)
                for h in late_hooks:
                    hook(h, after)

            act.wait_ge(consts_in, 16)
            act.wait_ge(const_ready, 1)
            for h in HOOKS:
                hook(h, Job(0, 0, 0))
            each_job(act, main)

        @block.vector
        def _(dve):
            def hook(h, prev, after):
                if h == "fin" and prev is not None:
                    dve.wait_ge(turned, prev.J + 1)
                    at = bass.ds(prev.c * CH, CH)
                    nc.vector.scalar_tensor_tensor(out=x[:, at], in0=turn_bank[:, :], scalar=prev.y["coef"],
                                                   in1=x[:, at], op0=ALU.mult, op1=ALU.add).then_inc(x_done, 1)
                elif h == "stats":
                    if after.L:
                        wait(dve, x_done, after.J - NC + 1)
                    elif isinstance(after.c, int) and after.c == 0:
                        dve.wait_ge(first_in, 16)
                    else:
                        dve.wait_ge(rest_in, 16)
                    wait(dve, mean_done, after.J)
                    for t in range(NT):
                        ins = nc.vector.bn_stats(stats[:, t, :], x[:, bass.ds(after.c * CH + t * D, D)])
                    ins.then_inc(stats_done, 1)
                    dve.wait_ge(stats_done, after.J + 1)
                    wait(dve, z_done, after.J)
                    carry_wait()
                    for t in range(NT):
                        ins = nc.vector.bn_aggr(mean_var[:, t, :], stats[:, t, :])
                    ins.then_inc(mean_done, 1)
                elif h == "z":
                    dve.wait_ge(rstd_done, after.J + 1)
                    wait(dve, zT_done, after.J)
                    for t in range(NT):
                        ins = nc.vector.tensor_scalar(z_tok[:, t, :], x[:, bass.ds(after.c * CH + t * D, D)],
                                                      mean_var[:, t, 0:1], rstd[:, t:t + 1], ALU.subtract, ALU.mult)
                    ins.then_inc(z_done, 1)
                elif h == "zsplit":
                    dve.wait_ge(zhi_done, after.J + 1)
                    nc.vector.tensor_tensor(z_lo[:, after.u, :], turn_bank[:, :], z_hi[:, after.u, :].bitcast(F32),
                                            ALU.subtract).then_inc(zlo_done, 1)
                elif h == "r1":
                    route_first(after)
                elif h == "r2":
                    route_second(after)

            def carry_wait():
                nc.vector.tensor_copy(waited[:, :], minus_half[:, 0:1])

            def stepper(job, start):
                count = [start]

                def step(ins):
                    count[0] += 1
                    ins.then_inc(route_step, 1)
                    dve.wait_ge(route_step, job.rsteps + count[0])
                return step, count

            def over(a, w):
                return a.broadcast_to([P, NT, w])

            def route_first(job):
                kind = job.y["route"]
                step, count = stepper(job, 0)
                dve.wait_ge(back_done, job.R + 1)
                step(nc.vector.tensor_copy(lg[:, :, :], route_bank[:, :].rearrange("p (t e) -> p t e", t=NT)[:, :, 0:16]))
                if kind != "grouped":
                    if kind == "softmax_dense":
                        nc.vector.tensor_reduce(r_sum[:, :, 1:2], lg[:, :, 8:10], AX.X, ALU.max)
                    carry_wait()
                    for t in range(NT):
                        ins = nc.vector.max(top8[:, t, :], lg[:, t, 0:8])
                    step(ins)
                    if kind == "softmax_dense":
                        nc.vector.tensor_tensor(masked[:, :, 8:10], lg[:, :, 8:10], over(r_sum[:, :, 1:2], 2), ALU.subtract)
                    step(nc.vector.tensor_tensor(masked[:, :, 0:8], lg[:, :, 0:8], over(top8[:, :, 0:1], 8), ALU.subtract))
                assert count[0] == R_BEFORE_EXP[kind]

            def chosen(step, values, w, out, k):
                carry_wait()
                for t in range(NT):
                    ins = nc.vector.max_index(at8[:, t, :], top8[:, t, :], values[:, t, :])
                step(ins)
                step(nc.vector.tensor_copy(at8f[:, :, :], at8[:, :, :]))
                iota = const("iota", P, 0, w)
                for t in range(NT):
                    ins = nc.vector.tensor_tensor(hit[:, t, 0:w, 0:k], iota.rearrange("p (w o) -> p w o", o=1).broadcast_to([P, w, k]),
                                                  at8f[:, t:t + 1, 0:k].broadcast_to([P, w, k]), ALU.is_equal)
                step(ins)
                step(nc.vector.tensor_reduce(out, hit[:, :, 0:w, 0:k], AX.X, ALU.add))

            def route_second(job):
                kind = job.y["route"]
                step, count = stepper(job, R_BEFORE_EXP[kind])
                dve.wait_ge(exp_done, job.R + 1)
                w = 16 if kind == "grouped" else 8
                if kind == "grouped":
                    step(nc.vector.tensor_tensor(lg[:, :, :], ex[:, :, :],
                                                 const("bias2").rearrange("p (o e) -> p o e", o=1).broadcast_to([P, NT, 16]), ALU.add))
                    v = lg[:, :, :].rearrange("p t (g m) -> p (t g) m", g=4)
                    s6 = pair6[:, :, :, :].rearrange("p t g m -> p (t g) m")
                    nc.vector.tensor_tensor(s6[:, :, 0:3], v[:, :, 0:3], v[:, :, 1:4], ALU.add)
                    nc.vector.tensor_tensor(s6[:, :, 3:5], v[:, :, 0:2], v[:, :, 2:4], ALU.add)
                    step(nc.vector.tensor_tensor(s6[:, :, 5:6], v[:, :, 0:1], v[:, :, 3:4], ALU.add))
                    step(nc.vector.tensor_reduce(groups[:, :, 0:4], pair6[:, :, :, :], AX.X, ALU.max))
                    carry_wait()
                    for t in range(NT):
                        ins = nc.vector.max(top8[:, t, :], groups[:, t, :])
                    step(ins)
                    chosen(step, groups, 4, gmask[:, :, :], 2)
                    g4 = gmask[:, :, :].rearrange("p t (g o) -> p (t g) o", o=1).broadcast_to([P, NT * 4, 4])
                    nc.vector.tensor_scalar(gfill[:, :, :], gmask[:, :, :], 1.0, -NEG, ALU.subtract, ALU.mult)
                    step(nc.vector.tensor_tensor(masked[:, :, :].rearrange("p t (g m) -> p (t g) m", g=4), v, g4, ALU.mult))
                    f4 = gfill[:, :, :].rearrange("p t (g o) -> p (t g) o", o=1).broadcast_to([P, NT * 4, 4])
                    mv = masked[:, :, :].rearrange("p t (g m) -> p (t g) m", g=4)
                    step(nc.vector.tensor_tensor(mv, mv, f4, ALU.add))
                    carry_wait()
                    for t in range(NT):
                        ins = nc.vector.max(top8[:, t, :], masked[:, t, :])
                    step(ins)
                    chosen(step, masked, 16, mask[:, :, 0:16], 4)
                else:
                    chosen(step, lg[:, :, 0:8], 8, mask[:, :, 0:8], 2)
                step(nc.vector.tensor_tensor(mask[:, :, 0:w], mask[:, :, 0:w], ex[:, :, 0:w], ALU.mult))
                if kind == "softmax_dense":
                    nc.vector.tensor_reduce(r_sum[:, :, 1:2], ex[:, :, 8:10], AX.X, ALU.add)
                step(nc.vector.tensor_reduce(r_sum[:, :, 0:1], mask[:, :, 0:w], AX.X, ALU.add))
                if kind == "grouped":
                    step(nc.vector.tensor_scalar(r_sum[:, :, 0:1], r_sum[:, :, 0:1], 1e-20, None, ALU.add))
                n = 2 if kind == "softmax_dense" else 1
                step(nc.vector.reciprocal(r_sum[:, :, 0:n], r_sum[:, :, 0:n]))
                if kind == "softmax_dense":
                    nc.vector.tensor_tensor(mask[:, :, 8:10], ex[:, :, 8:10], over(r_sum[:, :, 1:2], 2), ALU.mult)
                    step(nc.vector.tensor_tensor(mask[:, :, 0:8], mask[:, :, 0:8], over(r_sum[:, :, 0:1], 8), ALU.mult))
                    nc.vector.tensor_copy(cw[:, :, 8:9], mask[:, :, 9:10])
                    step(nc.vector.tensor_tensor(cw[:, :, 0:8], mask[:, :, 0:8], over(mask[:, :, 8:9], 8), ALU.mult))
                else:
                    scale = 2.5 if kind == "grouped" else 1.0
                    step(nc.vector.scalar_tensor_tensor(out=cw[:, :, 0:w], in0=mask[:, :, 0:w], scalar=scale,
                                                        in1=over(r_sum[:, :, 0:1], w), op0=ALU.mult, op1=ALU.mult))
                step(nc.vector.tensor_copy(cs_r[:, :, :], cw[:, :, :]))
                wait(dve, csT_done, job.R)
                nc.vector.tensor_copy(cs[:, :, 0:16], cs_r[:, :, :].bitcast(F32))
                step(nc.vector.tensor_tensor(cs[:, :, 16:32], cw[:, :, :], cs_r[:, :, :].bitcast(F32), ALU.subtract))
                assert count[0] == R_STEPS[kind], (kind, count[0])

            def tile(job, k):
                if k % 2 == 0:
                    dve.wait_ge(hi_by_act, job.half_tiles + k // 2 + 1)
                else:
                    dve.wait_ge(act_done, job.tiles + k + 1)
                    nc.vector.tensor_copy(h_hi[:, k % 3, :], hidden[:, k % 3, :]).then_inc(hi_by_dve, 1)
                    dve.wait_ge(hi_by_dve, job.half_tiles + k // 2 + 1)
                nc.vector.tensor_tensor(h_lo[:, k % 3, :], hidden[:, k % 3, :], h_hi[:, k % 3, :].bitcast(F32),
                                        ALU.subtract).then_inc(lo_done, 1)

            def scale_expert(job, e):
                y = job.y
                dve.wait_ge(y_done, job.experts + e + 1)
                b2 = const({"ff0": "b2_0", "ff1": "b2_1", "ff3": "b2_3"}[y["name"]], P, e, e + 1)
                if y["route"]:
                    dve.wait_ge(gain_done, job.gains + e + 1)
                    if e >= 2:
                        wait(dve, added, job.adds + e - 2 + (e == 2))
                    else:
                        wait(dve, added, job.adds)
                    nc.vector.scalar_tensor_tensor(out=scaled[:, e % 2, :], in0=y_bank[e % 2][:, :], scalar=b2,
                                                   in1=gain[:, e % 2, :], op0=ALU.add, op1=ALU.mult).then_inc(scaled_done, 1)
                else:
                    wait(dve, turned, job.J)
                    nc.vector.tensor_scalar(yT[:, :], y_bank[e % 2][:, :], b2, None, ALU.add).then_inc(yT_done, 1)

            def main(job, prev, after):
                y = job.y
                if y["kind"] == "ffn":
                    per = y["n"] // y["ne"]
                    hooks = hooks_at(job, after)
                    for k in range(y["n"] + 2):
                        if k < y["n"]:
                            tile(job, k)
                        if k >= 2 and (k - 2) % per == per - 1:
                            scale_expert(job, (k - 2) // per)
                        if k < y["n"]:
                            for h in hooks[k]:
                                hook(h, prev, after)
                elif y["kind"] == "pattention":
                    n0 = PATS[job.L] + job.c
                    hooks = spread(hook_names(after), 6)
                    for i in range(2):
                        for h in hooks[i]:
                            hook(h, prev, after)
                    for k in range(4):
                        dve.wait_ge(pa_hi, n0 * NT + k + 1)
                        nc.vector.tensor_tensor(h_lo[:, k % 3, :], bank[4 + k % 2][:, :], h_hi[:, k % 3, :].bitcast(F32),
                                                ALU.subtract).then_inc(pa_lo, 1)
                        for h in hooks[2 + k]:
                            hook(h, prev, after)
                    dve.wait_ge(pa_y, n0 + 1)
                    wait(dve, turned, job.J)
                    nc.vector.tensor_copy(yT[:, :], bank[0][:, :]).then_inc(yT_done, 1)
                elif y["kind"] == "attention":
                    if y["heads"] == 1 and isinstance(job.c, int) and job.c == 0:
                        ternary_weights()
                    attention(job, prev, after)
                elif y["kind"] == "retention":
                    retention(job, prev, after)
                elif y["kind"] == "glu":
                    n0 = PAIRS[job.L] + job.c * y["n"]
                    hooks = hooks_at(job, after)
                    for k in range(y["n"]):
                        dve.wait_ge(silu_done, n0 + k + 1)
                        nc.vector.tensor_tensor(scaled[:, k % 2, :], scaled[:, k % 2, :], glu_bank(1, k)[:, :],
                                                ALU.mult).then_inc(glu_uv, 1)
                        if k >= 1:
                            glu_split(n0, k - 1)
                            for h in hooks[k - 1]:
                                hook(h, prev, after)
                    glu_split(n0, y["n"] - 1)
                    for h in hooks[-1]:
                        hook(h, prev, after)
                    dve.wait_ge(glu_y, GLUS[job.L] + job.c + 1)
                    wait(dve, turned, job.J)
                    nc.vector.tensor_copy(yT[:, :], bank[4][:, :]).then_inc(yT_done, 1)

            def glu_split(n0, k):
                dve.wait_ge(glu_hi, n0 + k + 1)
                nc.vector.tensor_tensor(h_lo[:, k % 3, :], hidden[:, k % 3, :], h_hi[:, k % 3, :].bitcast(F32),
                                        ALU.subtract).then_inc(glu_lo, 1)

            def ternary_weights():
                count = [0]

                def step(ins):
                    count[0] += 1
                    ins.then_inc(ternary_step, 1)
                    dve.wait_ge(ternary_step, count[0])

                dve.wait_ge(ternary_total, 1)
                step(nc.vector.tensor_scalar(w_size[:, 2:4], bank[7][:, 0:2], 1.0 / (4 * D * D), 1e-8, ALU.mult, ALU.max))
                nc.vector.tensor_scalar(w_size[:, 4:6], w_size[:, 2:4], 0.5, None, ALU.mult)
                step(nc.vector.tensor_scalar(w_size[:, 6:8], w_size[:, 2:4], -0.5, None, ALU.mult))
                for m in range(2):
                    w = stage[:, m, 0:512]
                    above, below = ternary[:, 2, :], ternary[:, 3, :]
                    used = ternary[:, m, :]
                    at = slice(512 * m, 512 * (m + 1))
                    nc.vector.tensor_scalar(above, w, w_size[:, 4 + m:5 + m], None, ALU.is_gt)
                    step(nc.vector.tensor_scalar(below, w, w_size[:, 6 + m:7 + m], None, ALU.is_lt))
                    step(nc.vector.tensor_tensor(used, above, below, ALU.subtract))
                    step(nc.vector.tensor_tensor(above, used, w, ALU.subtract))
                    step(nc.vector.tensor_tensor(used, above, w, ALU.add))
                    step(nc.vector.tensor_copy(w3_hi[:, at], used))
                    step(nc.vector.tensor_tensor(w3_lo[:, at], used, w3_hi[:, at].bitcast(F32), ALU.subtract))
                assert count[0] == TERNARY_STEPS

            def retention(job, prev, after):
                c = job.c
                if job_first(job):
                    nc.vector.memset(decay[:, :], GAMMA)
                    nc.vector.memset(moments[:, 0, :], 0.0).then_inc(rt_moment, 1)
                dve.wait_ge(rt_vhi, c + 1)
                nc.vector.tensor_tensor(h_lo[:, 0, :], bank[1][:, :], h_hi[:, 0, :].bitcast(F32), ALU.subtract).then_inc(rt_vlo, 1)
                dve.wait_ge(rt_vsum, c + 1)
                dve.wait_ge(rt_keys, c + 1)
                dve.wait_ge(rt_moment, c * 2 + 1)
                nc.vector.tensor_tensor(scaled[:, 0, :], bank[3][:, :], gain[:, 0, :], ALU.mult).then_inc(rt_kv, 1)
                dve.wait_ge(rt_kv, c + 1)
                for b in range(SEQ):
                    nc.vector.tensor_tensor(moments[:, 0, :], moments[:, 0, :], scaled[:, 0, b * T:(b + 1) * T],
                                            ALU.add).then_inc(rt_moment, 1)
                    dve.wait_ge(rt_moment, c * 2 + b + 2)
                if isinstance(c, int) and c == NC - 1:
                    retention_end(job)
                for h in hook_names(after):
                    hook(h, prev, after)

            def retention_end(job):
                nc.vector.tensor_tensor_scan(states[:, 1:T], decay[:, 1:T], moments[:, 0, 1:T], 0.0,
                                             ALU.mult, ALU.add).then_inc(rt_scan, 1)
                dve.wait_ge(rt_scan, 1)
                nc.vector.tensor_copy(states[:, 0:1], states[:, 1:2]).then_inc(rt_states, 1)
                dve.wait_ge(rt_states_t, 1)
                nc.vector.tensor_copy(states_t[:, :], bank[0][:, 0:T]).then_inc(rt_ready, 1)
                dve.wait_ge(rt_ready, 1)
                dve.wait_ge(rt_queries, NC)
                with dve.Fori(0, NC) as c:
                    J = job.L * NC + c
                    at = bass.ds(c * CH, CH)
                    dve.wait_ge(turned, J)
                    nc.vector.tensor_tensor(yT[:, :].rearrange("p (b t) -> p b t", b=SEQ),
                                            queries[:, at].rearrange("p (b t) -> p b t", b=SEQ),
                                            states_t[:, :].rearrange("p (o t) -> p o t", o=1).broadcast_to([P, SEQ, T]),
                                            ALU.mult).then_inc(yT_done, 1)
                    dve.wait_ge(turned, J + 1)
                    nc.vector.tensor_tensor(x[:, at], turn_bank[:, :], x[:, at], ALU.add).then_inc(x_done, 1)

            def attention(job, prev, after):
                y = job.y
                heads, per = y["heads"], y["per"]
                groups = SEQ * heads // per
                A = ATTS[job.L] + job.c
                G = GROUPS[job.L] + job.c * groups
                hooks, late_hooks = attention_hooks(job, after)
                scale = float(D // heads) ** -0.5
                values, turned_p = attention_buffers(job)
                dve.wait_ge(at_proj, A * 3 + 3)
                if heads > 1:
                    dve.wait_ge(zeroed, 1)
                for t in range(NT):
                    src = bank[2][:, t * P:(t + 1) * P]
                    if heads > 1:
                        out = values[:, t, :].rearrange("p (h s) -> p h s", h=HEADS)[:, :, 0:HD]
                        ins = nc.vector.tensor_tensor(out, src.rearrange("p (h s) -> p h s", h=HEADS),
                                                      const("bv").rearrange("p (h s) -> p h s", h=HEADS), ALU.add)
                    else:
                        ins = nc.vector.tensor_copy(values[:, t, :], src)
                ins.then_inc(at_v, 1)

                def turned_out(g):
                    dve.wait_ge(at_turned, G + g + 1)
                    wait(dve, at_pv, G + g - 1)
                    nc.vector.tensor_copy(turned_p[:, g % 2, 2 * per * P:3 * per * P], bank[5][:, 0:per * P]).then_inc(at_out_d, 1)

                for g in range(groups):
                    dve.wait_ge(at_scores, G + g + 1)
                    wait(dve, at_negmax, G + g - 1)
                    for qb in range(2):
                        keys = (qb + 1) * P
                        ins = nc.vector.tensor_reduce(row_max[:, g % 2, qb * per:(qb + 1) * per],
                                                      bank[2 * (g % 2) + qb][:, 0:per * keys].rearrange("p (h k) -> p h k", h=per),
                                                      AX.X, ALU.max)
                    ins.then_inc(at_max, 1)
                    dve.wait_ge(at_max, G + g + 1)
                    wait(dve, at_probs, G + g - 1)
                    nc.vector.tensor_scalar(neg_max[:, g % 2, 0:2 * per], row_max[:, g % 2, 0:2 * per], -scale, None,
                                            ALU.mult).then_inc(at_negmax, 1)
                    if g >= 1:
                        turned_out(g - 1)
                    for h in hooks[g]:
                        hook(h, prev, after)
                turned_out(groups - 1)
                dve.wait_ge(at_probs, G + groups)
                wait(dve, at_norm, A)
                nc.vector.reciprocal(inv_sum[:, :, 0:heads], row_sum[:, :, 0:heads]).then_inc(at_inv, 1)
                dve.wait_ge(at_inv, A + 1)
                dve.wait_ge(at_tok, A + 1)
                for t in range(NT):
                    ins = nc.vector.tensor_tensor(hidden[:, 0, t * P:(t + 1) * P].rearrange("p (h s) -> p h s", h=heads),
                                                  bank[4][:, t * P:(t + 1) * P].rearrange("p (h s) -> p h s", h=heads),
                                                  inv_sum[:, t, 0:heads].rearrange("p (h o) -> p h o", o=1).broadcast_to([P, heads, D // heads]),
                                                  ALU.mult)
                ins.then_inc(at_norm, 1)
                dve.wait_ge(at_hi, A + 1)
                nc.vector.tensor_tensor(h_lo[:, 0, :], bank[5][:, :], h_hi[:, 0, :].bitcast(F32), ALU.subtract).then_inc(at_lo, 1)
                dve.wait_ge(at_y, A + 1)
                if heads > 1:
                    nc.vector.tensor_scalar(yT[:, :], bank[0][:, :], const("bo"), None, ALU.add).then_inc(yT_done, 1)
                else:
                    nc.vector.tensor_copy(yT[:, :], bank[0][:, :]).then_inc(yT_done, 1)
                for h in late_hooks:
                    hook(h, prev, after)

            dve.wait_ge(const_ready, 1)
            dve.wait_ge(consts_in, 16)
            dve.wait_ge(sel_in, 16)
            nc.vector.tensor_copy(sel1[:, :, :].rearrange("p e m -> p (e m)"),
                                  hidden[0:32, :, :].rearrange("p a n -> p (a n)")[:, 0:9 * P]).then_inc(sel_ready, 1)
            nc.vector.tensor_copy(ident_b[:, :], ident)
            nc.vector.tensor_copy(cmask_b[:, :], const("cmask"))
            nc.vector.tensor_copy(ones_r[:, :], ones[:, :]).then_inc(setup_done, 1)
            first = Job(0, 0, 0)
            for h in ("stats", "z", "zsplit"):
                hook(h, None, first)
            for i, (src, at, n) in enumerate(FIRST):
                hi, lo = {"ws": (ws_hi, ws_lo), "w0": (w0_hi, w0_lo)}[src]
                dve.wait_ge(first_piece_in[i % 2], 16 * (i // 2 + 1))
                nc.vector.tensor_copy(hi[:, at:at + n], stage[:, i % 2, 0:n]).then_inc(first_piece_hi, 1)
                dve.wait_ge(first_piece_hi, i + 1)
                nc.vector.tensor_tensor(lo[:, at:at + n], stage[:, i % 2, 0:n], hi[:, at:at + n].bitcast(F32),
                                        ALU.subtract).then_inc(first_piece_split, 1)
                if i == 0:
                    hook("r1", None, first)
                    hook("r2", None, first)
            each_job(dve, main)
            last = Job(NL - 1, NC - 1, 1)
            hook("fin", last, None)

        @block.tensor
        def _(pe):
            def product(out, w, z, start, stop):
                (w_hi, w_lo), (a_hi, a_lo) = w, z
                nc.tensor.matmul(out, w_hi, a_hi, start=start, stop=False)
                nc.tensor.matmul(out, w_hi, a_lo, start=False, stop=False)
                return nc.tensor.matmul(out, w_lo, a_hi, start=False, stop=stop)

            def hook(h, prev, after):
                if h == "fin" and prev is not None:
                    if prev.y["kind"] == "ffn" and prev.y["route"]:
                        pe.wait_ge(added, prev.adds + prev.y["ne"] - 1)
                    else:
                        pe.wait_ge(yT_done, YT[prev.L] + prev.c + 1)
                    wait(pe, zlo_done, prev.J + (1 if job_is_last(prev) else 2))
                    for t in range(NT):
                        ins = nc.tensor.transpose(turn_bank[:, t * P:(t + 1) * P], yT[:, t * P:(t + 1) * P], ident)
                    ins.then_inc(turned, 1)
                elif h == "zT":
                    pe.wait_ge(z_done, after.J + 1)
                    if after.y["kind"] == "retention" and not job_first(after):
                        pe.wait_ge(x_done, after.L * NC)
                    else:
                        wait(pe, x_done, after.J - 1)
                    for t in range(NT):
                        ins = nc.tensor.transpose(turn_bank[:, t * P:(t + 1) * P], z_tok[:, t, :], ident)
                    ins.then_inc(zT_done, 1)
                elif h == "logits":
                    pe.wait_ge(zlo_done, after.J + 1)
                    wait(pe, cT_done, after.R)
                    product(route_bank[:, :], router(after), z_of(after), True, True).then_inc(logits_done, 1)
                elif h == "back":
                    pe.wait_ge(const_ready, 1)
                    pe.wait_ge(lgT_done, after.R + 1)
                    for t in range(NT):
                        ins = nc.tensor.transpose(route_bank[:, t * P:(t + 1) * P], lgT[:, t * P:(t + 1) * P], ident)
                    ins.then_inc(back_done, 1)
                elif h == "cs":
                    pe.wait_ge(route_step, after.rsteps + R_STEPS[after.y["route"]])
                    for t in range(NT):
                        ins = nc.tensor.transpose(route_bank[0:32, t * P:(t + 1) * P], cs[:, t, :], ident)
                    ins.then_inc(csT_done, 1)

            def z_of(job):
                return z_hi[:, job.u, :], z_lo[:, job.u, :]

            def up(job, k):
                first_piece(job, k)
                wait(pe, act_done, job.tiles + (k - 2 if k >= 3 else 0))
                product(h_bank[k % 3][:, :], weights(job, "w1", k), z_of(job), True, True).then_inc(up_done, 1)

            def first_piece(job, k):
                if job.L == 0 and isinstance(job.c, int) and job.c == 0 and k % 2 == 0:
                    pe.wait_ge(first_piece_split, 2 + k // 2)

            def gain_bc(job, e):
                wait(pe, gain_done, job.gains + e)
                nc.tensor.matmul(gain_bank[:, :], sel1[:, e, :], cT[:, job.u, :], start=True, stop=True).then_inc(gain_mm, 1)

            def down(job, k):
                per = job.y["n"] // job.y["ne"]
                e = k // per
                pe.wait_ge(lo_done, job.tiles + k + 1)
                if k % per == 0:
                    if job.y["route"]:
                        wait(pe, scaled_done, job.gains + (e - 1 if e >= 2 else 0))
                    else:
                        wait(pe, yT_done, YT[job.L] + job.c)
                ins = product(y_bank[e % 2][:, :], weights(job, "w2", k), (h_hi[:, k % 3, :], h_lo[:, k % 3, :]),
                              k % per == 0, k % per == per - 1)
                if k % per == per - 1:
                    ins.then_inc(y_done, 1)

            def main(job, prev, after):
                y = job.y
                pe.wait_ge(zlo_done, job.J + 1)
                if y["kind"] == "ffn":
                    per = y["n"] // y["ne"]
                    hooks = hooks_at(job, after)
                    if y["route"]:
                        pe.wait_ge(cT_done, job.R + 1)
                    if job.L and layers[job.L - 1]["kind"] != "ffn":
                        quiet(job)
                    if y["name"] == "ff3" and job_first(job):
                        pe.wait_ge(ternary_step, TERNARY_STEPS)
                    for k in range(3):
                        up(job, k)
                    for k in range(y["n"]):
                        if y["route"] and k % per == 0:
                            gain_bc(job, k // per)
                        down(job, k)
                        if k + 3 < y["n"]:
                            up(job, k + 3)
                        for h in hooks[k]:
                            hook(h, prev, after)
                elif y["kind"] == "pattention":
                    pattention(job, prev, after)
                elif y["kind"] == "attention":
                    if y["heads"] == 1 and isinstance(job.c, int) and job.c == 0:
                        pe.wait_ge(ternary_sum, 2)
                        wait(pe, cT_done, ROUTED[job.L])
                        nc.tensor.matmul(bank[7][:, 0:2], ones[:, :], w_size[:, 0:2], start=True, stop=True).then_inc(ternary_total, 1)
                    attention(job, prev, after)
                elif y["kind"] == "glu":
                    glu(job, prev, after)
                elif y["kind"] == "retention":
                    retention(job, prev, after)

            def retention(job, prev, after):
                c = job.c
                quiet(job)
                wait(pe, rt_kv, c)
                wait(pe, rt_queries, c)
                product(bank[0][:, :], late("wk3"), z_of(job), True, True).then_inc(rt_proj, 1)
                product(bank[1][:, :], late("wv3"), z_of(job), True, True).then_inc(rt_proj, 1)
                product(bank[2][:, :], late("wq3"), z_of(job), True, True).then_inc(rt_proj, 1)
                pe.wait_ge(rt_vlo, c + 1)
                nc.tensor.matmul(bank[3][:, :], ones_r[:, :], h_hi[:, 0, :], start=True, stop=False)
                nc.tensor.matmul(bank[3][:, :], ones_r[:, :], h_lo[:, 0, :], start=False, stop=True).then_inc(rt_vsum, 1)
                if isinstance(c, int) and c == NC - 1:
                    pe.wait_ge(rt_states, 1)
                    for u in range(2):
                        ins = nc.tensor.transpose(bank[0][:, u * P:(u + 1) * P], states[:, u:T:2], ident)
                    ins.then_inc(rt_states_t, 1)
                    pe.wait_ge(zlo_done, job.J + 1)
                    with pe.Fori(0, NC) as i:
                        pe.wait_ge(yT_done, i + (YT[job.L] + 1))
                        pe.wait_ge(x_done, i + job.L * NC)
                        for t in range(NT):
                            ins = nc.tensor.transpose(turn_bank[:, t * P:(t + 1) * P], yT[:, t * P:(t + 1) * P], ident)
                        ins.then_inc(turned, 1)
                for h in hook_names(after):
                    hook(h, prev, after)

            def quiet(job):
                if isinstance(job.c, int) and job.c == 0:
                    before_ = layers[job.L - 1]
                    if before_["kind"] == "ffn" and before_["route"]:
                        pe.wait_ge(scaled_done, GAINS[job.L])
                        pe.wait_ge(added, ADDS[job.L])
                    else:
                        wait(pe, yT_done, YT[job.L])

            def z_tile(job, t):
                return z_hi[:, job.u, t * P:(t + 1) * P], z_lo[:, job.u, t * P:(t + 1) * P]

            def pattention(job, prev, after):
                n0 = PATS[job.L] + job.c
                hooks = spread(hook_names(after), 6)
                if isinstance(job.c, int) and job.c == 0:
                    pe.wait_ge(first_piece_split, len(FIRST))
                quiet(job)
                wait(pe, yT_done, YT[job.L] + job.c)
                for t in range(NT):
                    product(bank[t][:, :], z_tile(job, t), small("key"), True, True).then_inc(pa_logits, 1)
                for i in range(2):
                    for h in hooks[i]:
                        hook(h, prev, after)
                for k in range(4):
                    pe.wait_ge(pa_gelu, n0 * NT + NT)
                    if k >= 2:
                        pe.wait_ge(pa_lo, n0 * NT + k - 1)
                    elif k < 2:
                        wait(pe, pa_lo, n0 * NT)
                    for t in range(NT):
                        ins = nc.tensor.transpose(bank[4 + k % 2][:, t * P:(t + 1) * P], pat_rows(t)[:, k * P:(k + 1) * P], ident)
                    ins.then_inc(pa_turned, 1)
                    if k >= 1:
                        pat_down(n0, k - 1)
                    for h in hooks[2 + k]:
                        hook(h, prev, after)
                pat_down(n0, 3)

            def pat_down(n0, k):
                pe.wait_ge(pa_lo, n0 * NT + k + 1)
                ins = product(bank[0][:, :], small("value", k * P, (k + 1) * P), (h_hi[:, k % 3, :], h_lo[:, k % 3, :]), k == 0, k == 3)
                if k == 3:
                    ins.then_inc(pa_y, 1)

            def glu(job, prev, after):
                n = job.y["n"]
                n0 = PAIRS[job.L] + job.c * n
                hooks = hooks_at(job, after)
                quiet(job)
                pe.wait_ge(cT_done, job.R + 1)

                def pair(k):
                    if k >= 2:
                        pe.wait_ge(glu_uv, n0 + k - 1)
                    else:
                        wait(pe, glu_uv, n0)
                    product(glu_bank(0, k)[:, :], late("gate", k * P, (k + 1) * P), z_of(job), True, True)
                    product(glu_bank(1, k)[:, :], late("up", k * P, (k + 1) * P), z_of(job), True, True).then_inc(glu_mm, 1)
                    wait(pe, gain_done, job.gains + k)
                    sel = late("sel2", k * P, (k + 1) * P)[0]
                    nc.tensor.matmul(gain_bank[:, :], sel[0:32, :], cT[:, job.u, :], start=True, stop=True).then_inc(gain_mm, 1)

                pair(0)
                pair(1)
                for k in range(n):
                    pe.wait_ge(glu_lo, n0 + k + 1)
                    if k == 0:
                        wait(pe, yT_done, YT[job.L] + job.c)
                    ins = product(bank[4][:, :], late("down", k * P, (k + 1) * P), (h_hi[:, k % 3, :], h_lo[:, k % 3, :]), k == 0, k == n - 1)
                    if k == n - 1:
                        ins.then_inc(glu_y, 1)
                    if k + 2 < n:
                        pair(k + 2)
                    for h in hooks[k]:
                        hook(h, prev, after)

            def attention(job, prev, after):
                y = job.y
                heads, per = y["heads"], y["per"]
                groups = SEQ * heads // per
                A = ATTS[job.L] + job.c
                G = GROUPS[job.L] + job.c * groups
                hooks, late_hooks = attention_hooks(job, after)
                values, turned_p = attention_buffers(job)
                quiet(job)
                wait(pe, yT_done, YT[job.L] + job.c)
                w = small if heads > 1 else late
                n = "1" if heads > 1 else "2"
                product(bank[0][:, :], w("wq" + n), z_of(job), True, True).then_inc(at_proj, 1)
                product(bank[1][:, :], w("wk" + n), z_of(job), True, True).then_inc(at_proj, 1)
                for t in range(NT):
                    ins = product(bank[2][:, t * P:(t + 1) * P], z_tile(job, t), w("wv" + n), True, True)
                ins.then_inc(at_proj, 1)
                pe.wait_ge(at_qk, A * 2 + 2)
                if isinstance(job.c, int) and job.c == 0:
                    pe.wait_ge(setup_done, 1)

                def scores(g):
                    b = g // (groups // SEQ)
                    if heads > 1:
                        pe.wait_ge(at_keys, G - (GROUPS[job.L] if heads > 1 else 0) + g + 1)
                        keys = gain[:, g % 2, :].rearrange("p (h t) -> p h t", h=per)
                    else:
                        keys = scaled[:, 1, b * T:(b + 1) * T].rearrange("p (h t) -> p h t", h=1)
                    wait(pe, at_probs, G + g - 1)
                    if g == 1:
                        pe.wait_ge(at_v, A + 1)
                    for qb in range(2):
                        out = bank[2 * (g % 2) + qb][:, 0:per * (qb + 1) * P].rearrange("p (h k) -> p h k", h=per)
                        q = scaled[:, 0, b * T + qb * P:b * T + (qb + 1) * P]
                        nc.tensor.matmul(out, q, keys[:, :, 0:(qb + 1) * P], start=True, stop=False, skip_group_check=True)
                        ins = nc.tensor.matmul(out[:, :, qb * P:(qb + 1) * P], ident_b[:, :],
                                               cmask_b[:, :].rearrange("p (o k) -> p o k", o=1).broadcast_to([P, per, P]),
                                               start=False, stop=True, skip_group_check=True)
                    ins.then_inc(at_scores, 1)

                def turn(g):
                    pe.wait_ge(at_probs, G + g + 1)
                    wait(pe, at_out_a, G + g)
                    wait(pe, at_out_d, G + g)
                    probs = hidden[:, :, :].rearrange("p a n -> p (a n)").rearrange("p (s n) -> p s n", s=2)[:, g % 2, :]
                    for h in range(per):
                        nc.tensor.transpose(bank[4][:, 2 * h * P:(2 * h + 1) * P], probs[:, h * P:(h + 1) * P], ident)
                        at = per * P + h * 2 * P
                        nc.tensor.transpose(bank[4][:, (2 * h + 1) * P:(2 * h + 2) * P], probs[:, at:at + P], ident)
                        ins = nc.tensor.transpose(bank[5][:, h * P:(h + 1) * P], probs[:, at + P:at + 2 * P], ident)
                    ins.then_inc(at_turned, 1)

                def weigh(g):
                    b, hp = g // (groups // SEQ), g % (groups // SEQ)
                    pe.wait_ge(at_out_a, G + g + 1)
                    pe.wait_ge(at_out_d, G + g + 1)
                    for h in range(per):
                        at = (hp * per + h) * D
                        head = hp * per + h
                        nc.tensor.matmul(bank[7][:, b * T:(b + 1) * T], values[:, 2 * b, at:at + D],
                                         turned_p[:, g % 2, 2 * h * P:(2 * h + 2) * P],
                                         start=head == 0, stop=False, skip_group_check=True)
                        ins = nc.tensor.matmul(bank[7][:, b * T + P:(b + 1) * T], values[:, 2 * b + 1, at:at + D],
                                               turned_p[:, g % 2, (2 * per + h) * P:(2 * per + h + 1) * P],
                                               start=False, stop=head == heads - 1, skip_group_check=True)
                    ins.then_inc(at_pv, 1)

                pe.wait_ge(at_v, A + 1)
                wait(pe, cT_done, job_routed(job))
                scores(0)
                for g in range(groups):
                    if g + 1 < groups:
                        scores(g + 1)
                    turn(g)
                    if g >= 1:
                        weigh(g - 1)
                    for h in hooks[g]:
                        hook(h, prev, after)
                weigh(groups - 1)
                pe.wait_ge(at_raw, A + 1)
                for t in range(NT):
                    ins = nc.tensor.transpose(bank[4][:, t * P:(t + 1) * P], yT[:, t * P:(t + 1) * P], ident)
                ins.then_inc(at_tok, 1)
                pe.wait_ge(at_norm, A + 1)
                for t in range(NT):
                    ins = nc.tensor.transpose(bank[5][:, t * P:(t + 1) * P], hidden[:, 0, t * P:(t + 1) * P], ident)
                ins.then_inc(at_back, 1)
                pe.wait_ge(at_lo, A + 1)
                product(bank[0][:, :], w("wo" + n), (h_hi[:, 0, :], h_lo[:, 0, :]), True, True).then_inc(at_y, 1)
                for h in late_hooks:
                    hook(h, prev, after)

            def job_routed(job):
                return ROUTED[job.L]

            pe.wait_ge(consts_in, 16)
            pe.wait_ge(sel_ready, 1)
            first = Job(0, 0, 0)
            hook("zT", None, first)
            pe.wait_ge(first_piece_split, 1)
            for h in ("logits", "back", "cs"):
                hook(h, None, first)
            each_job(pe, main)
            hook("fin", Job(NL - 1, NC - 1, 1), None)


def kernel(**inputs):
    import concourse.bacc as _bacc
    from concourse.bass_utils import run_bass_kernel_spmd as _run

    nc = _bacc.Bacc("TRN2", target_bir_lowering=False, num_devices=1)
    arrays = lay_out({k: np.asarray(v) for k, v in inputs.items()})
    args = [nc.dram_tensor(n, a.shape, F32, kind="ExternalInput").ap() for n, a in arrays.items()]
    args.append(nc.dram_tensor("x_out", (B, T, D), F32, kind="ExternalOutput").ap())
    twelve_sublayers(nc, *args)
    r = _run(nc, [arrays], core_ids=[0])
    return r.results[0]["x_out"]


def lay_out(i):
    def hidden_tiles(w):
        w = w.reshape(-1, P, D)
        return w.transpose(1, 0, 2).reshape(P, -1)

    w1, w2 = i["L0_ffn_w1"], i["L0_ffn_w2"]
    w0 = np.concatenate([a for e in range(8) for a in (w1[e].T, hidden_tiles(w2[e].T))], axis=1)
    zero = np.zeros((P, P), np.float32)

    def router(*ws):
        w = np.concatenate(ws, axis=1)
        return np.concatenate([w, zero[:, w.shape[1]:]], axis=1)

    ws = np.concatenate([router(i["L0_ffn_router_w"].T), router(i["L1_ffn_Wg"], i["L1_ffn_Wr"]),
                         i["L0_attn_key_param_tokens"].T, hidden_tiles(i["L0_attn_value_param_tokens"]),
                         i["L1_attn_Wq"].T, i["L1_attn_Wk"].T, i["L1_attn_Wv"].T, i["L1_attn_Wo"].T], axis=1)
    wb = np.concatenate([i["L1_ffn_W1"].transpose(1, 0, 2).reshape(P, -1), i["L1_ffn_D1"],
                         hidden_tiles(i["L1_ffn_W2"]), hidden_tiles(i["L1_ffn_D2"])], axis=1)
    sel2 = np.zeros((P, 8, P), np.float32)
    for r in range(32):
        e = r % 16
        sel2[r, e // 2, 64 * (e % 2):64 * (e % 2) + 64] = 1.0
    wa = np.concatenate([i["L2_ffn_w_gate"].transpose(2, 0, 1).reshape(P, -1),
                         i["L2_ffn_w_up"].transpose(2, 0, 1).reshape(P, -1),
                         hidden_tiles(i["L2_ffn_w_down"].transpose(0, 2, 1)), router(i["L2_ffn_router_weight"].T),
                         sel2.reshape(P, -1), i["L2_attn_Wq"], i["L2_attn_Wk"], i["L2_attn_Wv"], i["L2_attn_Wo"],
                         i["L3_attn_Wq"], i["L3_attn_Wk"], i["L3_attn_Wv"], zero], axis=1)
    w3 = np.concatenate([i["L3_ffn_W1"].T, hidden_tiles(i["L3_ffn_W2"].T)], axis=1)

    cst = {n: np.zeros((P, w), np.float32) for n, (_, w) in C_COLS.items()}
    cst["ident"] = np.eye(P, dtype=np.float32)
    sel1 = np.zeros((32, 9, P), np.float32)
    for e in range(9):
        sel1[e, e] = sel1[16 + e, e] = 1.0
    cst["iota"][:] = np.arange(16, dtype=np.float32)
    cst["bias2"][:] = i["L2_ffn_router_bias"]
    cst["b1_0"][:] = i["L0_ffn_b1"].reshape(-1, P).T
    cst["b2_0"][:] = i["L0_ffn_b2"].T
    cst["b1_1"][:, 0:32] = i["L1_ffn_b1"].reshape(-1, P).T
    cst["b1_1"][:, 32:36] = i["L1_ffn_d1b"].reshape(-1, P).T
    cst["b2_1"][:, 0:8] = i["L1_ffn_b2"].T
    cst["b2_1"][:, 8] = i["L1_ffn_d2b"]
    cst["b1_3"][:] = i["L3_ffn_b1"].reshape(-1, P).T
    cst["b2_3"][:, 0] = i["L3_ffn_b2"]
    cst["rb1"][0:8, 0] = i["L1_ffn_bg"]
    cst["rb1"][8:10, 0] = i["L1_ffn_br"]
    cst["bq"][:, 0] = i["L1_attn_bq"]
    cst["bk"][:, 0] = i["L1_attn_bk"]
    cst["bo"][:, 0] = i["L1_attn_bo"]
    cst["bv"][:] = i["L1_attn_bv"]
    for h in range(HEADS):
        cst["hmask"][h * HD:(h + 1) * HD, h] = 1.0
    rows = np.arange(P)
    cst["cmask"][:] = np.where(rows[None, :] > rows[:, None], np.float32(LOWEST), np.float32(0.0))
    out = {"x": i["L0_attn_inputs"], "w0": w0, "ws": ws, "wb": wb, "wa": wa, "w3": w3,
           "cst": np.concatenate([cst[n] for n in C_COLS], axis=1), "sel": sel1.reshape(32, -1)}
    return {f"in_{k}": np.ascontiguousarray(v) for k, v in out.items()}
```

```python
from contextlib import ExitStack

import numpy as np

import concourse.bass as bass
from concourse import mybir

F32 = mybir.dt.float32
F32R = mybir.dt.float32r
U32 = mybir.dt.uint32
BF16 = mybir.dt.bfloat16
ALU = mybir.AluOpType
ACT = mybir.ActivationFunctionType
AX = mybir.AxisListType

P = 128
D = 128
B, T = 16, 256
TOK = B * T
CH = 512
NT = CH // P
NC = TOK // CH
SEQ = CH // T
LN_EPS = 1e-5
NEG = -1e9
LOWEST = -3.0e38
HEADS = 16
HD = D // HEADS
GAMMA = 0.96875

FF0 = dict(kind="ffn", name="ff0", n=16, ne=8, act=ACT.Gelu, route="softmax", coef=0.5)
PAT = dict(kind="pattention", name="pat", n=4, ne=1, act=ACT.Gelu, route=None, coef=1.0)
FF1 = dict(kind="ffn", name="ff1", n=36, ne=9, act=ACT.Relu, route="softmax_dense", coef=0.5)
AT1 = dict(kind="attention", name="at1", n=0, ne=0, act=None, route=None, coef=1.0, heads=16, per=2)
GLU = dict(kind="glu", name="glu", n=8, ne=8, act=ACT.Silu, route="grouped", coef=0.5)
AT2 = dict(kind="attention", name="at2", n=0, ne=0, act=None, route=None, coef=1.0, heads=1, per=1)
FF3 = dict(kind="ffn", name="ff3", n=4, ne=1, act=ACT.Gelu, route=None, coef=0.5)
RET = dict(kind="retention", name="ret", n=0, ne=0, act=None, route=None, coef=1.0)
LAYERS = [FF0, PAT, FF0, FF1, AT1, FF1, GLU, AT2, GLU, FF3, RET, FF3]

def columns(parts):
    at, out = 0, {}
    for name, width in parts:
        out[name] = (at, width)
        at += width
    return out, at


W0_COLS, W0_N = columns([(f"{w}{e}", 256) for e in range(8) for w in ("w1_", "w2_")])
WS_COLS, WS_N = columns([("router0", D), ("router1", D), ("key", 512), ("value", 512),
                         ("wq1", D), ("wk1", D), ("wv1", D), ("wo1", D)])
WB_COLS, WB_N = columns([("w1", 36 * D), ("w2", 36 * D)])
WA_COLS, WA_N = columns([("gate", 8 * D), ("up", 8 * D), ("down", 8 * D), ("router2", D), ("sel2", 8 * D),
                         ("wq2", D), ("wk2", D), ("wv2", D), ("wo2", D),
                         ("wq3", D), ("wk3", D), ("wv3", D), ("pad", D)])
W3_N = 8 * D
B_PIECE = WB_N // (3 * NC)
A_PIECE = WA_N // NC
assert B_PIECE * 3 * NC == WB_N and A_PIECE * NC == WA_N
C_COLS, C_N = columns([("ident", P), ("iota", 16), ("bias2", 16), ("b1_0", 16), ("b2_0", 8),
                       ("b1_1", 36), ("b2_1", 9), ("b1_3", 4), ("b2_3", 1), ("rb0", 1), ("rb1", 1), ("rb2", 1),
                       ("bq", 1), ("bk", 1), ("bo", 1), ("bv", D), ("hmask", HEADS), ("cmask", P)])

HOOKS = ["stats", "z", "zT", "zsplit", "fin", "logits", "logitsT", "back", "r1", "rx", "r2a", "r2b", "r2c", "r2d", "cs", "cT"]
PE_AT = {"zT": 2, "logits": 5, "fin": 5, "back": 7}
TILE_AT = {"stats": 0, "z": 2, "zsplit": 5, "logitsT": 8, "fin": 8, "r1": 9, "rx": 11,
           "r2a": 11, "r2b": 12, "r2c": 14, "r2d": 14}
LAST_AT = {FF0["n"]: {"cs": 13, "cT": 15}, FF1["n"]: {"cs": 14, "cT": 17}}
DENSE_PE_AT = {"zT": 1, "fin": 2}
DENSE_TILE_AT = {"stats": 0, "z": 1, "zsplit": 3, "fin": 3}
GAIN_LAG, SCALE_LAG = 2, 2

R_STEPS = {"softmax": 13, "softmax_dense": 14, "grouped": 23}
TERNARY_STEPS = 14
R_BEFORE_EXP = {"softmax": 3, "softmax_dense": 3, "grouped": 1}
R_WIDTH = {"softmax": 8, "softmax_dense": 10, "grouped": 16}
FIRST = [("ws", 0, 256)] + [("w0", i * 512, 512) for i in range(8)] + [("ws", 256 + i * 512, 512) for i in range(3)]
START = ["stats", "z", "zsplit", 0, "logitsT", 1, 2, "r1", 3, "rx", "r2a", 4, "r2b", "r2c", "r2d", "cT"]
PIECE_AFTER_TILE = {2 * i - 9: i for i in range(5, len(FIRST))}


GLU_AT = {"stats": 0, "z": 1, "zT": 1, "zsplit": 2, "logits": 2, "fin": 3, "logitsT": 3, "back": 3, "r1": 4, "rx": 5,
          "r2a": 5, "r2b": 5, "r2c": 6, "r2d": 6, "cs": 6, "cT": 6}
assert all(k < GLU["n"] - 1 for k in GLU_AT.values())


def twelve_sublayers(nc, x_in, w0, ws, wb, wa, w3, cst, sel, x_out, layers=LAYERS):
    NL = len(layers)
    with ExitStack() as ctx:
        def sb(name, shape, dt=F32):
            return ctx.enter_context(nc.sbuf_tensor(name, shape, dt))

        def sem(name):
            return ctx.enter_context(nc.semaphore(name))

        x = sb("x", [P, TOK])
        z_hi, z_lo = sb("z_hi", [P, 2, CH], F32R), sb("z_lo", [P, 2, CH], F32R)
        ws_hi, ws_lo = sb("ws_hi", [P, WS_N], F32R), sb("ws_lo", [P, WS_N], F32R)
        with nc.sbuf_tensor("values2", [P, NT, D], F32) as values2, nc.sbuf_tensor("turned_p2", [P, 2, 6 * P], F32) as turned_p2, \
                nc.sbuf_tensor("queries", [P, TOK], F32) as queries, nc.sbuf_tensor("moments", [P, 2, T], F32) as moments, \
                nc.sbuf_tensor("decay", [P, T], F32) as decay, nc.sbuf_tensor("states", [P, T], F32) as states, \
                nc.sbuf_tensor("states_t", [P, T], F32) as states_t, nc.sbuf_tensor("ternary", [P, 4, 512], F32) as ternary, \
                nc.sbuf_tensor("w3_hi", [P, W3_N], F32R) as w3_hi, nc.sbuf_tensor("w3_lo", [P, W3_N], F32R) as w3_lo:
            pass
        wb_hi, wb_lo = sb("wb_hi", [P, WB_N], F32R), sb("wb_lo", [P, WB_N], F32R)
        with nc.sbuf_tensor("w0_hi", [P, W0_N], F32R) as w0_hi, nc.sbuf_tensor("w0_lo", [P, W0_N], F32R) as w0_lo:
            pass
        with nc.sbuf_tensor("values1", [P, NT, HEADS * (D + HD)], F32) as values1, nc.sbuf_tensor("turned_p1", [P, 2, 6 * P], F32) as turned_p1:
            pass
        wa_hi, wa_lo = sb("wa_hi", [P, WA_N], F32R), sb("wa_lo", [P, WA_N], F32R)
        sel1 = sb("sel1", [32, 9, P], F32R)
        stage = sb("stage", [P, 2, A_PIECE])
        consts = sb("consts", [P, C_N])
        hidden = sb("hidden", [P, 3, CH])
        h_hi, h_lo = sb("h_hi", [P, 3, CH], F32R), sb("h_lo", [P, 3, CH], F32R)
        gain = sb("gain", [P, 2, CH])
        scaled = sb("scaled", [P, 2, CH])
        yT = sb("yT", [P, CH])
        z_tok = sb("z_tok", [P, NT, D])
        stats = sb("stats", [P, NT, 6])
        mean_var = sb("mean_var", [P, NT, 2])
        var_eps = sb("var_eps", [P, NT])
        rstd = sb("rstd", [P, NT])
        minus_half = sb("minus_half", [P, NT])
        eps, per_key = sb("eps", [P, NT]), sb("per_key", [P, NT])
        lgT = sb("lgT", [P, CH])
        lg = sb("lg", [P, NT, 16])
        ex = sb("ex", [P, NT, 16])
        top8 = sb("top8", [P, NT, 8])
        at8 = sb("at8", [P, NT, 8], U32)
        at8f = sb("at8f", [P, NT, 8])
        mask = sb("mask", [P, NT, 16])
        hit = sb("hit", [P, NT, 16, 4])
        r_sum = sb("r_sum", [P, NT, 2])
        cw = sb("cw", [P, NT, 16])
        cs = sb("cs", [P, NT, 32])
        cs_r = sb("cs_r", [P, NT, 16], F32R)
        groups = sb("groups", [P, NT, 8])
        gmask = sb("gmask", [P, NT, 4])
        gfill = sb("gfill", [P, NT, 4])
        masked = sb("masked", [P, NT, 16])
        pair6 = sb("pair6", [P, NT, 4, 6])
        cT = sb("cT", [32, 2, CH], F32R)
        norm = sb("norm", [P, NT])
        row_max = sb("row_max", [P, 2, 4])
        neg_max = sb("neg_max", [P, 2, 4])
        row_sum = sb("row_sum", [P, NT, HEADS])
        inv_sum = sb("inv_sum", [P, NT, HEADS])
        ones_r = sb("ones_r", [P, P], F32R)
        ones = sb("ones", [P, P])
        waited = sb("waited", [P, 1])
        ident_b, cmask_b = sb("ident_b", [P, P], BF16), sb("cmask_b", [P, P], BF16)
        w_size = sb("w_size", [P, 8])

        def const(name, rows=P, lo=0, hi=None):
            a, w = C_COLS[name]
            return consts[0:rows, a + lo:a + (w if hi is None else hi)]

        ident = const("ident")

        bank = [ctx.enter_context(nc.psum_tensor(f"bank{i}", [P, CH], F32)) for i in range(8)]
        h_bank = [bank[0], bank[1], bank[4]]
        y_bank = [bank[2], bank[3]]
        gain_bank = bank[5]
        turn_bank = bank[6]
        route_bank = bank[7]

        first_in, consts_in, rest_in = sem("first_in"), sem("consts_in"), sem("rest_in")
        first_piece_in = [sem("first_piece_in0"), sem("first_piece_in1")]
        first_piece_hi, first_piece_split = sem("first_piece_hi"), sem("first_piece_split")
        piece_in = [sem("piece_in0"), sem("piece_in1")]
        piece_hi, piece_split = sem("piece_hi"), sem("piece_split")
        sel_in, sel_ready = sem("sel_in"), sem("sel_ready")
        x_stored = sem("x_stored")
        const_ready = sem("const_ready")
        stats_done, mean_done, eps_added, rstd_done = sem("stats_done"), sem("mean_done"), sem("eps_added"), sem("rstd_done")
        z_done, zT_done, zhi_done, zlo_done = sem("z_done"), sem("zT_done"), sem("zhi_done"), sem("zlo_done")
        logits_done, lgT_done, back_done = sem("logits_done"), sem("lgT_done"), sem("back_done")
        route_step, exp_done, csT_done, cT_done = sem("route_step"), sem("exp_done"), sem("csT_done"), sem("cT_done")
        up_done, act_done = sem("up_done"), sem("act_done")
        hi_by_act, hi_by_dve, lo_done = sem("hi_by_act"), sem("hi_by_dve"), sem("lo_done")
        gain_mm, gain_done = sem("gain_mm"), sem("gain_done")
        y_done, scaled_done = sem("y_done"), sem("scaled_done")
        added = sem("added")
        yT_done, turned, x_done = sem("yT_done"), sem("turned"), sem("x_done")
        pa_logits, pa_squares, pa_mean, pa_norm, pa_gelu = sem("pa_logits"), sem("pa_squares"), sem("pa_mean"), sem("pa_norm"), sem("pa_gelu")
        pa_turned, pa_hi, pa_lo, pa_y = sem("pa_turned"), sem("pa_hi"), sem("pa_lo"), sem("pa_y")
        at_proj, at_qk, at_v, at_keys = sem("at_proj"), sem("at_qk"), sem("at_v"), sem("at_keys")
        at_scores, at_max, at_negmax, at_probs = sem("at_scores"), sem("at_max"), sem("at_negmax"), sem("at_probs")
        at_turned, at_out_a, at_out_d, at_pv = sem("at_turned"), sem("at_out_a"), sem("at_out_d"), sem("at_pv")
        at_raw, at_tok, at_inv, at_norm, at_back, at_hi, at_lo, at_y = [sem(n) for n in (
            "at_raw", "at_tok", "at_inv", "at_norm", "at_back", "at_hi", "at_lo", "at_y")]
        glu_mm, silu_done, glu_uv, glu_h, glu_hi, glu_lo, glu_y = [sem(n) for n in (
            "glu_mm", "silu_done", "glu_uv", "glu_h", "glu_hi", "glu_lo", "glu_y")]
        zeroed = sem("zeroed")
        setup_done = sem("setup_done")
        ternary_sum, ternary_total, ternary_step = sem("ternary_sum"), sem("ternary_total"), sem("ternary_step")
        rt_proj, rt_keys, rt_vhi, rt_queries, rt_vlo, rt_vsum, rt_kv, rt_moment = [sem(n) for n in (
            "rt_proj", "rt_keys", "rt_vhi", "rt_queries", "rt_vlo", "rt_vsum", "rt_kv", "rt_moment")]
        rt_scan, rt_states, rt_states_t, rt_ready = sem("rt_scan"), sem("rt_states"), sem("rt_states_t"), sem("rt_ready")

        def wait(eng, s, value):
            if isinstance(value, int) and value <= 0:
                return
            eng.wait_ge(s, value)

        def before(L, f):
            return sum(f(layers[i]) for i in range(L)) * NC

        TILES = [before(L, lambda y: y["n"] if y["kind"] in ("ffn",) else 0) for L in range(NL + 1)]
        ROUTED = [before(L, lambda y: 1 if y["route"] else 0) for L in range(NL + 1)]
        EXPERTS = [before(L, lambda y: y["ne"] if y["kind"] in ("ffn",) else 0) for L in range(NL + 1)]
        GAINS = [before(L, lambda y: y["ne"] if y["route"] else 0) for L in range(NL + 1)]
        ADDS = [before(L, lambda y: y["ne"] - 1 if y["kind"] == "ffn" and y["route"] else 0) for L in range(NL + 1)]
        PAIRS = [before(L, lambda y: y["n"] if y["kind"] == "glu" else 0) for L in range(NL + 1)]
        GLUS = [before(L, lambda y: 1 if y["kind"] == "glu" else 0) for L in range(NL + 1)]
        PATS = [before(L, lambda y: 1 if y["kind"] == "pattention" else 0) for L in range(NL + 1)]
        ATTS = [before(L, lambda y: 1 if y["kind"] == "attention" else 0) for L in range(NL + 1)]
        GROUPS = [before(L, lambda y: SEQ * y["heads"] // y["per"] if y["kind"] == "attention" else 0) for L in range(NL + 1)]
        RSTEPS = [before(L, lambda y: R_STEPS[y["route"]] if y["route"] else 0) for L in range(NL + 1)]

        class Job:

            def __init__(self, L, c, u, pair=0):
                self.L, self.c, self.u, self.pair, self.y = L, c, u, pair, layers[L]
                self.J = L * NC + c
                self.R = ROUTED[L] + c
                n, ne = self.y["n"], self.y["ne"]
                self.tiles = TILES[L] + c * n
                self.half_tiles = TILES[L] // 2 + c * (n // 2)
                self.experts = EXPERTS[L] + c * ne
                self.gains = GAINS[L] + c * ne
                self.adds = ADDS[L] + c * (ne - 1)
                self.rsteps = RSTEPS[L] + c * R_STEPS.get(self.y["route"], 0)

        def job_first(job):
            return isinstance(job.c, int) and job.c == 0

        def job_is_last(job):
            return job.L == NL - 1 and isinstance(job.c, int) and job.c == NC - 1

        def joined(job):
            return job.y["kind"] != "retention" and not job_first(job)

        def slot(job, k):
            return (k + (job.u if job.y["n"] % 3 else 0)) % 3

        def turn(job, e):
            return (e + (job.u if job.y["ne"] % 2 else 0)) % 2

        def tile_before(job, k):
            if k >= 3 or joined(job) and (job.y["n"] % 3 == 0 or job.u == 1):
                return job.tiles + k - 2
            return job.tiles

        def behind(job, prev, k, lag):
            if k >= lag:
                return job, k - lag
            if joined(job):
                return prev, prev.y["n"] + k - lag
            return None, 0

        def tail(job, after, lag):
            return 0 if after is not None and joined(after) else lag

        YT = [before(L, lambda y: 0 if y["kind"] == "ffn" and y["route"] else 1) for L in range(NL + 1)]

        def each_job(eng, main):
            for L in range(NL):
                def pair(c0, number):
                    for u in range(2):
                        c = c0 + u
                        job = Job(L, c, u, number)
                        if u == 1:
                            prev = Job(L, c0, 0)
                        elif isinstance(c0, int) and c0 == 0:
                            prev = Job(L - 1, NC - 1, 1) if L else None
                        else:
                            prev = Job(L, c0 - 1, 1)
                        if prev is not None and prev.y["kind"] == "retention":
                            prev = None
                        if isinstance(c, int) and c == NC - 1:
                            after = Job(L + 1, 0, 0) if L + 1 < NL else None
                        else:
                            after = Job(L, c + 1, 1 - u)
                        main(job, prev, after)
                pair(0, 0)
                with eng.Fori(1, NC // 2 - 1) as i:
                    pair(i * 2, i)
                pair(NC - 2, NC // 2 - 1)

        def hook_names(after):
            names = list(HOOKS) if after is not None else ["fin"]
            return names if after is None or after.y["route"] else names[:5]

        def spread(names, points):
            out = [[] for _ in range(points)]
            for i, h in enumerate(names):
                out[min(points - 1, i * points // len(names))].append(h)
            return out

        def retention_hooks(job, after):
            names = hook_names(after)
            return (names[:4], names[4:]) if after is not None and after.L == job.L else ([], names)

        def attention_hooks(job, after):
            groups = SEQ * job.y["heads"] // job.y["per"]
            names = hook_names(after)
            if groups == 2:
                return [[h for h in names[:5] if h != "fin"], ["fin"]], names[5:]
            return spread(names[:5], groups), names[5:]

        def hooks_at(job, after, places):
            names = hook_names(after)
            n = job.y["n"]
            if job.y["kind"] == "glu":
                at = GLU_AT
            elif job.y["route"]:
                at = {**places, **LAST_AT[n]}
            else:
                at = DENSE_PE_AT if places is PE_AT else DENSE_TILE_AT
            return [[h for h in names if at.get(h) == k] for k in range(n)]

        def weights(job, part, k):
            name = job.y["name"]
            if name == "ff0":
                a = W0_COLS[f"{part}_{k // 2}"][0] + (k % 2) * P
                return w0_hi[:, a:a + P], w0_lo[:, a:a + P]
            if name == "ff3":
                a = (0 if part == "w1" else 512) + k * P
                return w3_hi[:, a:a + P], w3_lo[:, a:a + P]
            if name == "ff1":
                a = WB_COLS[part][0] + k * P
                return wb_hi[:, a:a + P], wb_lo[:, a:a + P]
            raise ValueError(name)

        def small(name, lo=0, hi=None):
            a, w = WS_COLS[name]
            s = slice(a + lo, a + (w if hi is None else hi))
            return ws_hi[:, s], ws_lo[:, s]

        def late(name, lo=0, hi=None):
            a, w = WA_COLS[name]
            s = slice(a + lo, a + (w if hi is None else hi))
            return wa_hi[:, s], wa_lo[:, s]

        def router(job):
            return {"ff0": lambda: small("router0"), "ff1": lambda: small("router1"),
                    "glu": lambda: late("router2")}[job.y["name"]]()


        def pat_rows(t):
            return hidden[:, t, :] if t < 3 else gain[:, 0, :]

        def pat_out(after):
            return bank[7] if after is not None and joined(after) else bank[0]

        def glu_bank(which, k):
            return bank[2 * (k % 2) + which]

        def normalised():
            return lgT[:, :]

        def attention_buffers(job):
            return (values1, turned_p1) if job.y["heads"] > 1 else (values2, turned_p2)

        block = ctx.enter_context(nc.Block())

        @block.sync
        def _(sp):
            xv = x[:, :].rearrange("p (t d) -> p t d", d=D)
            xd = x_in.rearrange("b (t p) d -> p (b t) d", p=P)
            od = x_out.rearrange("b (t p) d -> p (b t) d", p=P)
            sp.dma_start(xv[:, 0:NT, :], xd[:, 0:NT, :]).then_inc(first_in, 16)
            sp.dma_start(consts[:, :], cst).then_inc(consts_in, 16)
            sp.dma_start(hidden[0:32, :, :].rearrange("p a n -> p (a n)")[:, 0:9 * P], sel).then_inc(sel_in, 16)
            for i, (src, at, n) in enumerate(FIRST):
                if i >= 2:
                    sp.wait_ge(first_piece_split, i - 1)
                sp.dma_start(stage[:, i % 2, 0:n], {"ws": ws, "w0": w0}[src][:, at:at + n]).then_inc(first_piece_in[i % 2], 16)
                if i == 1:
                    sp.dma_start(xv[:, NT:, :], xd[:, NT:, :]).then_inc(rest_in, 16)
            if NL > 3:
                sp.wait_ge(first_piece_split, len(FIRST))
                for n in range(2):
                    sp.dma_start(stage[:, n, 0:B_PIECE], wb[:, n * B_PIECE:(n + 1) * B_PIECE]).then_inc(piece_in[n], 16)
                with sp.Fori(1, 3 * NC // 2) as i:
                    for u in range(2):
                        sp.wait_ge(piece_split, i * 2 + (u - 1))
                        sp.dma_start(stage[:, u, 0:B_PIECE],
                                     wb[:, bass.ds(i * (2 * B_PIECE) + u * B_PIECE, B_PIECE)]).then_inc(piece_in[u], 16)
            if NL > 6:
                for n in range(NC):
                    sp.wait_ge(piece_split, 3 * NC + n - 1)
                    sp.dma_start(stage[:, n % 2, 0:A_PIECE], wa[:, n * A_PIECE:(n + 1) * A_PIECE]).then_inc(piece_in[n % 2], 16)
                for n in range(2):
                    sp.wait_ge(piece_split, 4 * NC + n - 1)
                    sp.dma_start(stage[:, n, 0:512], w3[:, n * 512:(n + 1) * 512]).then_inc(piece_in[n], 16)
            early = (NC - 2) * NT
            sp.wait_ge(x_done, NL * NC - 2)
            sp.dma_start(od[:, 0:early, :], xv[:, 0:early, :]).then_inc(x_stored, 16)
            sp.wait_ge(x_done, NL * NC)
            sp.dma_start(od[:, early:, :], xv[:, early:, :]).then_inc(x_stored, 16)
            sp.wait_ge(x_stored, 32)

        @block.gpsimd
        def _(pool):
            nc.gpsimd.memset(minus_half[:, :], -0.5)
            nc.gpsimd.memset(eps[:, :], LN_EPS)
            nc.gpsimd.memset(per_key[:, :], 1.0 / 512)
            nc.gpsimd.memset(ones[:, :], 1.0)
            nc.gpsimd.memset(cw[:, :, :], 0.0)
            nc.gpsimd.memset(lgT[:, :], 0.0)
            nc.gpsimd.memset(groups[:, :, :], LOWEST).then_inc(const_ready, 1)
            pool.wait_ge(const_ready, 1)

            def rstd_of(job):
                pool.wait_ge(mean_done, job.J + 1)
                nc.gpsimd.tensor_tensor(var_eps[:, :], mean_var[:, :, 1], eps[:, :], ALU.add).then_inc(eps_added, 1)
                pool.wait_ge(eps_added, job.J + 1)
                wait(pool, z_done, job.J)
                nc.gpsimd.tensor_tensor(rstd[:, :], var_eps[:, :], minus_half[:, :], ALU.pow).then_inc(rstd_done, 1)

            def split_piece(number, slot, of_slot, hi, lo, n):
                w = stage[:, slot, 0:n]
                pool.wait_ge(piece_in[slot], of_slot * 16)
                nc.gpsimd.tensor_copy(hi, w).then_inc(piece_hi, 1)
                pool.wait_ge(piece_hi, number + 1)
                nc.gpsimd.tensor_tensor(lo, w, hi.bitcast(F32), ALU.subtract).then_inc(piece_split, 1)

            def weights_ahead(job):
                if job.L < 3 and NL > 3:
                    at = bass.ds(job.J * B_PIECE, B_PIECE)
                    split_piece(job.J, job.u, (job.L * NC // 2) + job.pair + 1, wb_hi[:, at], wb_lo[:, at], B_PIECE)
                if job.L == 5 and NL > 6:
                    at = bass.ds(job.c * A_PIECE, A_PIECE)
                    split_piece(job.c + 3 * NC, job.u, (3 * NC // 2) + job.pair + 1, wa_hi[:, at], wa_lo[:, at], A_PIECE)

            def add_expert(job, e):
                pool.wait_ge(scaled_done, job.gains + e + 1)
                if e == 1:
                    wait(pool, turned, job.J)
                    a = scaled[:, turn(job, 0), :]
                else:
                    pool.wait_ge(added, job.adds + e - 1)
                    a = yT[:, :]
                nc.gpsimd.tensor_tensor(yT[:, :], a, scaled[:, turn(job, e), :], ALU.add).then_inc(added, 1)

            def main(job, prev, after):
                y = job.y
                if y["kind"] == "ffn":
                    per = y["n"] // y["ne"]
                    hooks = hooks_at(job, after, TILE_AT)
                    for k in range(y["n"] + tail(job, after, SCALE_LAG)):
                        of, tile = behind(job, prev, k, SCALE_LAG)
                        if y["route"] and of is not None and tile % per == per - 1 and tile >= per:
                            add_expert(of, tile // per)
                        if k < y["n"] and "stats" in hooks[k]:
                            rstd_of(after)
                        if k == (y["n"] - 1 if job.L == 0 and job_first(job) else min(4, y["n"] - 1)):
                            weights_ahead(job)
                elif y["kind"] == "pattention":
                    pool.wait_ge(pa_squares, (PATS[job.L] + job.c) * NT + NT)
                    nc.gpsimd.tensor_tensor(norm[:, :], norm[:, :], per_key[:, :], ALU.mult).then_inc(pa_mean, 1)
                    pool.wait_ge(pa_mean, PATS[job.L] + job.c + 1)
                    nc.gpsimd.tensor_tensor(norm[:, :], norm[:, :], minus_half[:, :], ALU.pow).then_inc(pa_norm, 1)
                    if after is not None:
                        rstd_of(after)
                    weights_ahead(job)
                elif y["kind"] == "attention":
                    keys_of_heads(job, after)
                elif y["kind"] == "retention":
                    if after is not None:
                        rstd_of(after)
                elif y["kind"] == "glu":
                    n0 = PAIRS[job.L] + job.c * y["n"]
                    hooks = hooks_at(job, after, None)
                    for k in range(y["n"]):
                        pool.wait_ge(glu_uv, n0 + k + 1)
                        pool.wait_ge(gain_done, job.gains + k + 1)
                        wait(pool, glu_lo, n0 + (k - 2 if k >= 3 else (-1, 0, -2)[k]))
                        nc.gpsimd.tensor_tensor(hidden[:, k % 3, :], scaled[:, k % 2, :], gain[:, k % 2, :], ALU.mult).then_inc(glu_h, 1)
                        if k >= 1 and "stats" in hooks[k - 1]:
                            rstd_of(after)

            def keys_of_heads(job, after):
                y = job.y
                groups = SEQ * y["heads"] // y["per"]
                hooks, late_hooks = attention_hooks(job, after)
                G = GROUPS[job.L] + job.c * groups
                if y["heads"] > 1 and isinstance(job.c, int) and job.c == 0:
                    pool.wait_ge(x_done, job.L * NC - 1)
                    nc.gpsimd.memset(values1[:, :, :], 0.0).then_inc(zeroed, 1)
                for g in range(groups):
                    if y["heads"] > 1:
                        b, hp = g // (groups // SEQ), g % (groups // SEQ)
                        if g == 0:
                            pool.wait_ge(at_qk, (ATTS[job.L] + job.c) * 2 + 2)
                        wait(pool, at_scores, G + g - 1)
                        pool_k = scaled[:, 1, b * T:(b + 1) * T].rearrange("p (o t) -> p o t", o=1).broadcast_to([P, 2, T])
                        hm = const("hmask", P, 2 * hp, 2 * hp + 2).rearrange("p (h o) -> p h o", o=1).broadcast_to([P, 2, T])
                        nc.gpsimd.tensor_tensor(gain[:, g % 2, :].rearrange("p (h t) -> p h t", h=2), pool_k, hm,
                                                ALU.mult).then_inc(at_keys, 1)
                    if "stats" in hooks[max(g - 1, 0)] and g >= 1:
                        rstd_of(after)

            rstd_of(Job(0, 0, 0))
            each_job(pool, main)

        @block.scalar
        def _(act):
            def hook(h, after):
                if h == "zsplit":
                    act.wait_ge(zT_done, after.J + 1)
                    nc.scalar.activation(z_hi[:, after.u, :], turn_bank[:, :], ACT.Copy).then_inc(zhi_done, 1)
                elif h == "logitsT":
                    act.wait_ge(logits_done, after.R + 1)
                    bias = {"ff0": "rb0", "ff1": "rb1", "glu": "rb2"}[after.y["name"]]
                    nc.scalar.activation(lgT[0:32, :], route_bank[0:32, :], ACT.Identity,
                                         bias=const(bias, 32)).then_inc(lgT_done, 1)
                elif h == "rx":
                    route = after.y["route"]
                    w = R_WIDTH[route]
                    act.wait_ge(route_step, after.rsteps + R_BEFORE_EXP[route])
                    src = lg if route == "grouped" else masked
                    nc.scalar.activation(ex[:, :, 0:w], src[:, :, 0:w],
                                         ACT.Sigmoid if route == "grouped" else ACT.Exp).then_inc(exp_done, 1)
                elif h == "cT":
                    act.wait_ge(csT_done, after.R + 1)
                    nc.scalar.activation(cT[:, after.u, :], route_bank[0:32, :], ACT.Copy).then_inc(cT_done, 1)

            def tile(job, k):
                y = job.y
                act.wait_ge(up_done, job.tiles + k + 1)
                wait(act, lo_done, tile_before(job, k))
                m = slot(job, k)
                bias = const({"ff0": "b1_0", "ff1": "b1_1", "ff3": "b1_3"}[y["name"]], P, k, k + 1)
                nc.scalar.activation(hidden[:, m, :], h_bank[m][:, :], y["act"], bias=bias).then_inc(act_done, 1)
                if k % 2 == 0:
                    act.wait_ge(act_done, job.tiles + k + 1)
                    nc.scalar.activation(h_hi[:, m, :], hidden[:, m, :], ACT.Copy).then_inc(hi_by_act, 1)

            def first_piece(i):
                src, at, n = FIRST[i]
                act.wait_ge(first_piece_in[i % 2], 16 * (i // 2 + 1))
                nc.scalar.activation({"ws": ws_hi, "w0": w0_hi}[src][:, at:at + n], stage[:, i % 2, 0:n],
                                     ACT.Copy).then_inc(first_piece_hi, 1)

            def dense_out(job):
                act.wait_ge(y_done, job.experts + 1)
                wait(act, turned, job.J)
                nc.scalar.activation(yT[:, :], y_bank[turn(job, 0)][:, :], ACT.Identity, bias=const("b2_3", P)).then_inc(yT_done, 1)

            def gain_of(job, e):
                act.wait_ge(gain_mm, job.gains + e + 1)
                wait(act, scaled_done, job.gains + e - 1)
                nc.scalar.activation(gain[:, turn(job, e), :], gain_bank[:, :], ACT.Copy).then_inc(gain_done, 1)

            def main(job, prev, after):
                y = job.y
                if y["kind"] == "ffn":
                    per = y["n"] // y["ne"]
                    hooks = hooks_at(job, after, TILE_AT)
                    for k in range(y["n"] + tail(job, after, GAIN_LAG)):
                        if k < y["n"]:
                            tile(job, k)
                        of, at = behind(job, prev, k, GAIN_LAG)
                        if y["route"] and of is not None and at % per == 0:
                            gain_of(of, at // per)
                        if not y["route"] and of is not None and at == y["n"] - 1:
                            dense_out(of)
                        if k < y["n"]:
                            for h in hooks[k]:
                                hook(h, after)
                            if job.L == 0 and job_first(job) and k in PIECE_AFTER_TILE:
                                first_piece(PIECE_AFTER_TILE[k])
                elif y["kind"] == "pattention":
                    n0 = PATS[job.L] + job.c
                    hooks = spread(hook_names(after), 6)
                    for h in hooks[0]:
                        hook(h, after)

                    def squares(n0):
                        for t in range(NT):
                            act.wait_ge(pa_logits, n0 * NT + t + 1)
                            if t == 0:
                                wait(act, pa_norm, n0)
                                wait(act, pa_turned, n0 * NT)
                                wait(act, pa_gelu, n0 * NT)
                            nc.scalar.activation(pat_rows(t), bank[t][:, :], ACT.Square,
                                                 accum_out=norm[:, t:t + 1]).then_inc(pa_squares, 1)

                    if not joined(job):
                        squares(n0)
                    for h in hooks[1]:
                        hook(h, after)
                    act.wait_ge(pa_norm, n0 + 1)
                    for t in range(NT):
                        nc.scalar.activation(pat_rows(t), bank[t][:, :], ACT.Gelu, scale=norm[:, t:t + 1]).then_inc(pa_gelu, 1)
                    for k in range(4):
                        act.wait_ge(pa_turned, n0 * NT + k + 1)
                        nc.scalar.activation(h_hi[:, k % 3, :], bank[4 + k % 2][:, :], ACT.Copy).then_inc(pa_hi, 1)
                        for h in hooks[2 + k]:
                            hook(h, after)
                    if after is not None and joined(after):
                        squares(n0 + 1)
                elif y["kind"] == "attention":
                    if y["heads"] == 1 and isinstance(job.c, int) and job.c == 0:
                        for m in range(2):
                            act.wait_ge(piece_in[m], 16 * (3 * NC // 2 + NC // 2 + 1))
                            nc.scalar.activation(ternary[:, m, :], stage[:, m, 0:512], ACT.Abs,
                                                 accum_out=w_size[:, m:m + 1]).then_inc(ternary_sum, 1)
                    attention(job, after)
                elif y["kind"] == "retention":
                    if job_first(job):
                        act.wait_ge(yT_done, YT[job.L])
                    act.wait_ge(rt_proj, job.c * 3 + 1)
                    wait(act, rt_kv, job.c)
                    nc.scalar.activation(gain[:, 0, :], bank[0][:, :], ACT.Copy).then_inc(rt_keys, 1)
                    act.wait_ge(rt_proj, job.c * 3 + 2)
                    nc.scalar.activation(h_hi[:, 0, :], bank[1][:, :], ACT.Copy).then_inc(rt_vhi, 1)
                    act.wait_ge(rt_proj, job.c * 3 + 3)
                    nc.scalar.activation(queries[:, bass.ds(job.c * CH, CH)], bank[2][:, :], ACT.Copy).then_inc(rt_queries, 1)
                    for names in retention_hooks(job, after):
                        for h in names:
                            hook(h, after)
                elif y["kind"] == "glu":
                    n0 = PAIRS[job.L] + job.c * y["n"]
                    hooks = hooks_at(job, after, None)
                    for k in range(y["n"]):
                        act.wait_ge(glu_mm, n0 + k + 1)
                        wait(act, glu_h, n0 + k - 1)
                        nc.scalar.activation(scaled[:, k % 2, :], glu_bank(0, k)[:, :], ACT.Silu).then_inc(silu_done, 1)
                        if k == 0 and joined(job):
                            glu_split(n0 - y["n"], y["n"] - 1)
                        act.wait_ge(gain_mm, job.gains + k + 1)
                        nc.scalar.activation(gain[:, k % 2, :], gain_bank[:, :], ACT.Copy).then_inc(gain_done, 1)
                        if k >= 1:
                            glu_split(n0, k - 1)
                            for h in hooks[k - 1]:
                                hook(h, after)
                    if tail(job, after, 1):
                        glu_split(n0, y["n"] - 1)

            def glu_split(n0, k):
                act.wait_ge(glu_h, n0 + k + 1)
                nc.scalar.activation(h_hi[:, k % 3, :], hidden[:, k % 3, :], ACT.Copy).then_inc(glu_hi, 1)

            def attention(job, after):
                y = job.y
                heads, per = y["heads"], y["per"]
                groups = SEQ * heads // per
                A = ATTS[job.L] + job.c
                G = GROUPS[job.L] + job.c * groups
                hooks, late_hooks = attention_hooks(job, after)
                scale = float(D // heads) ** -0.5
                probs = hidden[:, :, :].rearrange("p a n -> p (a n)").rearrange("p (s n) -> p s n", s=2)
                _, turned_p = attention_buffers(job)
                def queries_keys(job):
                    for i, name in enumerate(("bq", "bk")):
                        act.wait_ge(at_proj, (ATTS[job.L] + job.c) * 3 + i + 1)
                        if heads > 1:
                            nc.scalar.activation(scaled[:, i, :], bank[i][:, :], ACT.Identity, bias=const(name)).then_inc(at_qk, 1)
                        else:
                            nc.scalar.activation(scaled[:, i, :], bank[i][:, :], ACT.Copy).then_inc(at_qk, 1)

                if not joined(job):
                    queries_keys(job)

                def turned_out(g):
                    act.wait_ge(at_turned, G + g + 1)
                    wait(act, at_pv, G + g - 1)
                    nc.scalar.activation(turned_p[:, g % 2, 0:2 * per * P], bank[4][:, 0:2 * per * P], ACT.Copy).then_inc(at_out_a, 1)

                for g in range(groups):
                    b, hp = g // (groups // SEQ), g % (groups // SEQ)
                    act.wait_ge(at_negmax, G + g + 1)
                    wait(act, at_turned, G + g - 1)
                    if g == 0:
                        wait(act, at_inv, A)
                    for qb in range(2):
                        for h in range(per):
                            keys = (qb + 1) * P
                            at = h * P if qb == 0 else per * P + h * 2 * P
                            src = bank[2 * (g % 2) + qb][:, h * keys:(h + 1) * keys]
                            ins = nc.scalar.activation(probs[:, g % 2, at:at + keys], src, ACT.Exp,
                                                       bias=neg_max[:, g % 2, qb * per + h:qb * per + h + 1], scale=scale,
                                                       accum_out=row_sum[:, 2 * b + qb, hp * per + h:hp * per + h + 1])
                    ins.then_inc(at_probs, 1)
                    if g >= 1:
                        turned_out(g - 1)
                    for h in hooks[g]:
                        hook(h, after)
                turned_out(groups - 1)
                if after is not None and joined(after):
                    queries_keys(after)
                act.wait_ge(at_pv, G + groups)
                wait(act, turned, job.J)
                nc.scalar.activation(yT[:, :], bank[7][:, :], ACT.Copy).then_inc(at_raw, 1)
                act.wait_ge(at_back, A + 1)
                nc.scalar.activation(h_hi[:, 0, :], bank[5][:, :], ACT.Copy).then_inc(at_hi, 1)
                for h in late_hooks:
                    hook(h, after)

            act.wait_ge(consts_in, 16)
            act.wait_ge(const_ready, 1)
            for h in START:
                if isinstance(h, int):
                    first_piece(h)
                else:
                    hook(h, Job(0, 0, 0))
            each_job(act, main)

        @block.vector
        def _(dve):
            routing = []

            def hook(h, prev, after):
                if h == "fin" and prev is not None:
                    dve.wait_ge(turned, prev.J + 1)
                    at = bass.ds(prev.c * CH, CH)
                    nc.vector.scalar_tensor_tensor(out=x[:, at], in0=turn_bank[:, :], scalar=prev.y["coef"],
                                                   in1=x[:, at], op0=ALU.mult, op1=ALU.add).then_inc(x_done, 1)
                elif h == "stats":
                    if after.L:
                        wait(dve, x_done, after.J - NC + 1)
                    elif isinstance(after.c, int) and after.c == 0:
                        dve.wait_ge(first_in, 16)
                    else:
                        dve.wait_ge(rest_in, 16)
                    wait(dve, mean_done, after.J)
                    for t in range(NT):
                        ins = nc.vector.bn_stats(stats[:, t, :], x[:, bass.ds(after.c * CH + t * D, D)])
                    ins.then_inc(stats_done, 1)
                    dve.wait_ge(stats_done, after.J + 1)
                    wait(dve, z_done, after.J)
                    carry_wait()
                    for t in range(NT):
                        ins = nc.vector.bn_aggr(mean_var[:, t, :], stats[:, t, :])
                    ins.then_inc(mean_done, 1)
                elif h == "z":
                    dve.wait_ge(rstd_done, after.J + 1)
                    wait(dve, zT_done, after.J)
                    for t in range(NT):
                        ins = nc.vector.tensor_scalar(z_tok[:, t, :], x[:, bass.ds(after.c * CH + t * D, D)],
                                                      mean_var[:, t, 0:1], rstd[:, t:t + 1], ALU.subtract, ALU.mult)
                    ins.then_inc(z_done, 1)
                elif h == "zsplit":
                    dve.wait_ge(zhi_done, after.J + 1)
                    nc.vector.tensor_tensor(z_lo[:, after.u, :], turn_bank[:, :], z_hi[:, after.u, :].bitcast(F32),
                                            ALU.subtract).then_inc(zlo_done, 1)
                elif h == "r1":
                    route_first(after)
                elif h == "r2a":
                    routing.append(route_second(after))
                    next(routing[-1])
                elif h in ("r2b", "r2c"):
                    next(routing[-1])
                elif h == "r2d":
                    assert next(routing[-1], None) is None

            def carry_wait():
                nc.vector.tensor_copy(waited[:, :], minus_half[:, 0:1])

            def stepper(job, start):
                count = [start]

                def step(ins):
                    count[0] += 1
                    ins.then_inc(route_step, 1)
                    dve.wait_ge(route_step, job.rsteps + count[0])
                return step, count

            def over(a, w):
                return a.broadcast_to([P, NT, w])

            def route_first(job):
                kind = job.y["route"]
                step, count = stepper(job, 0)
                dve.wait_ge(back_done, job.R + 1)
                step(nc.vector.tensor_copy(lg[:, :, :], route_bank[:, :].rearrange("p (t e) -> p t e", t=NT)[:, :, 0:16]))
                if kind != "grouped":
                    if kind == "softmax_dense":
                        nc.vector.tensor_reduce(r_sum[:, :, 1:2], lg[:, :, 8:10], AX.X, ALU.max)
                    carry_wait()
                    for t in range(NT):
                        ins = nc.vector.max(top8[:, t, :], lg[:, t, 0:8])
                    step(ins)
                    if kind == "softmax_dense":
                        nc.vector.tensor_tensor(masked[:, :, 8:10], lg[:, :, 8:10], over(r_sum[:, :, 1:2], 2), ALU.subtract)
                    step(nc.vector.tensor_tensor(masked[:, :, 0:8], lg[:, :, 0:8], over(top8[:, :, 0:1], 8), ALU.subtract))
                assert count[0] == R_BEFORE_EXP[kind]

            def chosen(step, values, w, out, k):
                carry_wait()
                for t in range(NT):
                    ins = nc.vector.max_index(at8[:, t, :], top8[:, t, :], values[:, t, :])
                step(ins)
                step(nc.vector.tensor_copy(at8f[:, :, :], at8[:, :, :]))
                iota = const("iota", P, 0, w)
                for t in range(NT):
                    ins = nc.vector.tensor_tensor(hit[:, t, 0:w, 0:k], iota.rearrange("p (w o) -> p w o", o=1).broadcast_to([P, w, k]),
                                                  at8f[:, t:t + 1, 0:k].broadcast_to([P, w, k]), ALU.is_equal)
                step(ins)
                step(nc.vector.tensor_reduce(out, hit[:, :, 0:w, 0:k], AX.X, ALU.add))

            def route_second(job):
                kind = job.y["route"]
                step, count = stepper(job, R_BEFORE_EXP[kind])
                dve.wait_ge(exp_done, job.R + 1)
                w = 16 if kind == "grouped" else 8
                if kind == "grouped":
                    step(nc.vector.tensor_tensor(lg[:, :, :], ex[:, :, :],
                                                 const("bias2").rearrange("p (o e) -> p o e", o=1).broadcast_to([P, NT, 16]), ALU.add))
                    v = lg[:, :, :].rearrange("p t (g m) -> p (t g) m", g=4)
                    s6 = pair6[:, :, :, :].rearrange("p t g m -> p (t g) m")
                    nc.vector.tensor_tensor(s6[:, :, 0:3], v[:, :, 0:3], v[:, :, 1:4], ALU.add)
                    nc.vector.tensor_tensor(s6[:, :, 3:5], v[:, :, 0:2], v[:, :, 2:4], ALU.add)
                    step(nc.vector.tensor_tensor(s6[:, :, 5:6], v[:, :, 0:1], v[:, :, 3:4], ALU.add))
                    step(nc.vector.tensor_reduce(groups[:, :, 0:4], pair6[:, :, :, :], AX.X, ALU.max))
                    carry_wait()
                    for t in range(NT):
                        ins = nc.vector.max(top8[:, t, :], groups[:, t, :])
                    step(ins)
                    yield
                    chosen(step, groups, 4, gmask[:, :, :], 2)
                    g4 = gmask[:, :, :].rearrange("p t (g o) -> p (t g) o", o=1).broadcast_to([P, NT * 4, 4])
                    nc.vector.tensor_scalar(gfill[:, :, :], gmask[:, :, :], 1.0, -NEG, ALU.subtract, ALU.mult)
                    step(nc.vector.tensor_tensor(masked[:, :, :].rearrange("p t (g m) -> p (t g) m", g=4), v, g4, ALU.mult))
                    f4 = gfill[:, :, :].rearrange("p t (g o) -> p (t g) o", o=1).broadcast_to([P, NT * 4, 4])
                    mv = masked[:, :, :].rearrange("p t (g m) -> p (t g) m", g=4)
                    step(nc.vector.tensor_tensor(mv, mv, f4, ALU.add))
                    carry_wait()
                    for t in range(NT):
                        ins = nc.vector.max(top8[:, t, :], masked[:, t, :])
                    step(ins)
                    yield
                    chosen(step, masked, 16, mask[:, :, 0:16], 4)
                else:
                    chosen(step, lg[:, :, 0:8], 8, mask[:, :, 0:8], 2)
                    yield
                step(nc.vector.tensor_tensor(mask[:, :, 0:w], mask[:, :, 0:w], ex[:, :, 0:w], ALU.mult))
                if kind == "softmax_dense":
                    nc.vector.tensor_reduce(r_sum[:, :, 1:2], ex[:, :, 8:10], AX.X, ALU.add)
                step(nc.vector.tensor_reduce(r_sum[:, :, 0:1], mask[:, :, 0:w], AX.X, ALU.add))
                if kind == "grouped":
                    step(nc.vector.tensor_scalar(r_sum[:, :, 0:1], r_sum[:, :, 0:1], 1e-20, None, ALU.add))
                if kind != "grouped":
                    yield
                n = 2 if kind == "softmax_dense" else 1
                step(nc.vector.reciprocal(r_sum[:, :, 0:n], r_sum[:, :, 0:n]))
                if kind == "softmax_dense":
                    nc.vector.tensor_tensor(mask[:, :, 8:10], ex[:, :, 8:10], over(r_sum[:, :, 1:2], 2), ALU.mult)
                    step(nc.vector.tensor_tensor(mask[:, :, 0:8], mask[:, :, 0:8], over(r_sum[:, :, 0:1], 8), ALU.mult))
                    nc.vector.tensor_copy(cw[:, :, 8:9], mask[:, :, 9:10])
                    step(nc.vector.tensor_tensor(cw[:, :, 0:8], mask[:, :, 0:8], over(mask[:, :, 8:9], 8), ALU.mult))
                else:
                    scale = 2.5 if kind == "grouped" else 1.0
                    step(nc.vector.scalar_tensor_tensor(out=cw[:, :, 0:w], in0=mask[:, :, 0:w], scalar=scale,
                                                        in1=over(r_sum[:, :, 0:1], w), op0=ALU.mult, op1=ALU.mult))
                yield
                step(nc.vector.tensor_copy(cs_r[:, :, :], cw[:, :, :]))
                wait(dve, csT_done, job.R)
                nc.vector.tensor_copy(cs[:, :, 0:16], cs_r[:, :, :].bitcast(F32))
                step(nc.vector.tensor_tensor(cs[:, :, 16:32], cw[:, :, :], cs_r[:, :, :].bitcast(F32), ALU.subtract))
                assert count[0] == R_STEPS[kind], (kind, count[0])

            def tile(job, k):
                m = slot(job, k)
                if k % 2 == 0:
                    dve.wait_ge(hi_by_act, job.half_tiles + k // 2 + 1)
                else:
                    dve.wait_ge(act_done, job.tiles + k + 1)
                    nc.vector.tensor_copy(h_hi[:, m, :], hidden[:, m, :]).then_inc(hi_by_dve, 1)
                    dve.wait_ge(hi_by_dve, job.half_tiles + k // 2 + 1)
                nc.vector.tensor_tensor(h_lo[:, m, :], hidden[:, m, :], h_hi[:, m, :].bitcast(F32),
                                        ALU.subtract).then_inc(lo_done, 1)

            def first_piece(i):
                src, at, n = FIRST[i]
                hi, lo = {"ws": (ws_hi, ws_lo), "w0": (w0_hi, w0_lo)}[src]
                dve.wait_ge(first_piece_hi, i + 1)
                nc.vector.tensor_tensor(lo[:, at:at + n], stage[:, i % 2, 0:n], hi[:, at:at + n].bitcast(F32),
                                        ALU.subtract).then_inc(first_piece_split, 1)

            def scale_expert(job, e):
                y = job.y
                dve.wait_ge(y_done, job.experts + e + 1)
                b2 = const({"ff0": "b2_0", "ff1": "b2_1"}[y["name"]], P, e, e + 1)
                dve.wait_ge(gain_done, job.gains + e + 1)
                wait(dve, added, job.adds + (e - 1 if e < 2 else max(e - 2, 1)))
                m = turn(job, e)
                nc.vector.scalar_tensor_tensor(out=scaled[:, m, :], in0=y_bank[m][:, :], scalar=b2,
                                               in1=gain[:, m, :], op0=ALU.add, op1=ALU.mult).then_inc(scaled_done, 1)

            def main(job, prev, after):
                y = job.y
                if y["kind"] == "ffn":
                    per = y["n"] // y["ne"]
                    hooks = hooks_at(job, after, TILE_AT)
                    for k in range(y["n"] + tail(job, after, SCALE_LAG)):
                        if k < y["n"]:
                            tile(job, k)
                        of, at = behind(job, prev, k, SCALE_LAG)
                        if y["route"] and of is not None and at % per == per - 1:
                            scale_expert(of, at // per)
                        if k < y["n"]:
                            for h in hooks[k]:
                                hook(h, prev, after)
                            if job.L == 0 and job_first(job) and k in PIECE_AFTER_TILE:
                                first_piece(PIECE_AFTER_TILE[k])
                elif y["kind"] == "pattention":
                    n0 = PATS[job.L] + job.c
                    hooks = spread(hook_names(after), 6)
                    for i in range(2):
                        for h in hooks[i]:
                            hook(h, prev, after)
                    for k in range(4):
                        dve.wait_ge(pa_hi, n0 * NT + k + 1)
                        nc.vector.tensor_tensor(h_lo[:, k % 3, :], bank[4 + k % 2][:, :], h_hi[:, k % 3, :].bitcast(F32),
                                                ALU.subtract).then_inc(pa_lo, 1)
                        for h in hooks[2 + k]:
                            hook(h, prev, after)
                    dve.wait_ge(pa_y, n0 + 1)
                    wait(dve, turned, job.J)
                    nc.vector.tensor_copy(yT[:, :], pat_out(after)[:, :]).then_inc(yT_done, 1)
                elif y["kind"] == "attention":
                    if y["heads"] == 1 and isinstance(job.c, int) and job.c == 0:
                        ternary_weights()
                    attention(job, prev, after)
                elif y["kind"] == "retention":
                    retention(job, prev, after)
                elif y["kind"] == "glu":
                    n0 = PAIRS[job.L] + job.c * y["n"]
                    hooks = hooks_at(job, after, None)
                    for k in range(y["n"]):
                        dve.wait_ge(silu_done, n0 + k + 1)
                        nc.vector.tensor_tensor(scaled[:, k % 2, :], scaled[:, k % 2, :], glu_bank(1, k)[:, :],
                                                ALU.mult).then_inc(glu_uv, 1)
                        if k == 0 and joined(job):
                            glu_split(n0 - y["n"], y["n"] - 1)
                        if k == 1 and joined(job):
                            glu_out(prev)
                        if k >= 1:
                            glu_split(n0, k - 1)
                            for h in hooks[k - 1]:
                                hook(h, prev, after)
                    if tail(job, after, 1):
                        glu_split(n0, y["n"] - 1)
                        glu_out(job)

            def glu_out(job):
                dve.wait_ge(glu_y, GLUS[job.L] + job.c + 1)
                wait(dve, turned, job.J)
                nc.vector.tensor_copy(yT[:, :], bank[4][:, :]).then_inc(yT_done, 1)

            def glu_split(n0, k):
                dve.wait_ge(glu_hi, n0 + k + 1)
                nc.vector.tensor_tensor(h_lo[:, k % 3, :], hidden[:, k % 3, :], h_hi[:, k % 3, :].bitcast(F32),
                                        ALU.subtract).then_inc(glu_lo, 1)

            def ternary_weights():
                count = [0]

                def step(ins):
                    count[0] += 1
                    ins.then_inc(ternary_step, 1)
                    dve.wait_ge(ternary_step, count[0])

                dve.wait_ge(ternary_total, 1)
                step(nc.vector.tensor_scalar(w_size[:, 2:4], bank[7][:, 0:2], 1.0 / (4 * D * D), 1e-8, ALU.mult, ALU.max))
                nc.vector.tensor_scalar(w_size[:, 4:6], w_size[:, 2:4], 0.5, None, ALU.mult)
                step(nc.vector.tensor_scalar(w_size[:, 6:8], w_size[:, 2:4], -0.5, None, ALU.mult))
                for m in range(2):
                    w = stage[:, m, 0:512]
                    above, below = ternary[:, 2, :], ternary[:, 3, :]
                    used = ternary[:, m, :]
                    at = slice(512 * m, 512 * (m + 1))
                    nc.vector.tensor_scalar(above, w, w_size[:, 4 + m:5 + m], None, ALU.is_gt)
                    step(nc.vector.tensor_scalar(below, w, w_size[:, 6 + m:7 + m], None, ALU.is_lt))
                    step(nc.vector.tensor_tensor(used, above, below, ALU.subtract))
                    step(nc.vector.tensor_tensor(above, used, w, ALU.subtract))
                    step(nc.vector.tensor_tensor(used, above, w, ALU.add))
                    step(nc.vector.tensor_copy(w3_hi[:, at], used))
                    step(nc.vector.tensor_tensor(w3_lo[:, at], used, w3_hi[:, at].bitcast(F32), ALU.subtract))
                assert count[0] == TERNARY_STEPS

            def retention(job, prev, after):
                c = job.c
                if job_first(job):
                    nc.vector.memset(decay[:, :], GAMMA)
                    nc.vector.memset(moments[:, 0, :], 0.0).then_inc(rt_moment, 1)
                within, at_end = retention_hooks(job, after)
                for h in within[:2]:
                    hook(h, prev, after)
                dve.wait_ge(rt_vhi, c + 1)
                nc.vector.tensor_tensor(h_lo[:, 0, :], bank[1][:, :], h_hi[:, 0, :].bitcast(F32), ALU.subtract).then_inc(rt_vlo, 1)
                for h in within[2:]:
                    hook(h, prev, after)
                dve.wait_ge(rt_vsum, c + 1)
                dve.wait_ge(rt_keys, c + 1)
                dve.wait_ge(rt_moment, c * 2 + 1)
                nc.vector.tensor_tensor(scaled[:, 0, :], bank[3][:, :], gain[:, 0, :], ALU.mult).then_inc(rt_kv, 1)
                dve.wait_ge(rt_kv, c + 1)
                for b in range(SEQ):
                    nc.vector.tensor_tensor(moments[:, 0, :], moments[:, 0, :], scaled[:, 0, b * T:(b + 1) * T],
                                            ALU.add).then_inc(rt_moment, 1)
                    dve.wait_ge(rt_moment, c * 2 + b + 2)
                if isinstance(c, int) and c == NC - 1:
                    retention_end(job)
                for h in at_end:
                    hook(h, prev, after)

            def retention_end(job):
                nc.vector.tensor_tensor_scan(states[:, 1:T], decay[:, 1:T], moments[:, 0, 1:T], 0.0,
                                             ALU.mult, ALU.add).then_inc(rt_scan, 1)
                dve.wait_ge(rt_scan, 1)
                nc.vector.tensor_copy(states[:, 0:1], states[:, 1:2]).then_inc(rt_states, 1)
                dve.wait_ge(rt_states_t, 1)
                nc.vector.tensor_copy(states_t[:, :], bank[0][:, 0:T]).then_inc(rt_ready, 1)
                dve.wait_ge(rt_ready, 1)
                dve.wait_ge(rt_queries, NC)
                with dve.Fori(0, NC) as c:
                    J = job.L * NC + c
                    at = bass.ds(c * CH, CH)
                    dve.wait_ge(turned, J)
                    nc.vector.tensor_tensor(yT[:, :].rearrange("p (b t) -> p b t", b=SEQ),
                                            queries[:, at].rearrange("p (b t) -> p b t", b=SEQ),
                                            states_t[:, :].rearrange("p (o t) -> p o t", o=1).broadcast_to([P, SEQ, T]),
                                            ALU.mult).then_inc(yT_done, 1)
                    dve.wait_ge(turned, J + 1)
                    nc.vector.tensor_tensor(x[:, at], turn_bank[:, :], x[:, at], ALU.add).then_inc(x_done, 1)

            def attention(job, prev, after):
                y = job.y
                heads, per = y["heads"], y["per"]
                groups = SEQ * heads // per
                A = ATTS[job.L] + job.c
                G = GROUPS[job.L] + job.c * groups
                hooks, late_hooks = attention_hooks(job, after)
                scale = float(D // heads) ** -0.5
                values, turned_p = attention_buffers(job)
                if heads > 1:
                    dve.wait_ge(zeroed, 1)

                def values_out(job):
                    dve.wait_ge(at_proj, (ATTS[job.L] + job.c) * 3 + 3)
                    for t in range(NT):
                        src = bank[2][:, t * P:(t + 1) * P]
                        if heads > 1:
                            out = values[:, t, :].rearrange("p (h s) -> p h s", h=HEADS)[:, :, 0:HD]
                            ins = nc.vector.tensor_tensor(out, src.rearrange("p (h s) -> p h s", h=HEADS),
                                                          const("bv").rearrange("p (h s) -> p h s", h=HEADS), ALU.add)
                        else:
                            ins = nc.vector.tensor_copy(values[:, t, :], src)
                    ins.then_inc(at_v, 1)

                if not joined(job):
                    values_out(job)

                def turned_out(g):
                    dve.wait_ge(at_turned, G + g + 1)
                    wait(dve, at_pv, G + g - 1)
                    nc.vector.tensor_copy(turned_p[:, g % 2, 2 * per * P:3 * per * P], bank[5][:, 0:per * P]).then_inc(at_out_d, 1)

                for g in range(groups):
                    dve.wait_ge(at_scores, G + g + 1)
                    wait(dve, at_negmax, G + g - 1)
                    for qb in range(2):
                        keys = (qb + 1) * P
                        ins = nc.vector.tensor_reduce(row_max[:, g % 2, qb * per:(qb + 1) * per],
                                                      bank[2 * (g % 2) + qb][:, 0:per * keys].rearrange("p (h k) -> p h k", h=per),
                                                      AX.X, ALU.max)
                    ins.then_inc(at_max, 1)
                    dve.wait_ge(at_max, G + g + 1)
                    wait(dve, at_probs, G + g - 1)
                    nc.vector.tensor_scalar(neg_max[:, g % 2, 0:2 * per], row_max[:, g % 2, 0:2 * per], -scale, None,
                                            ALU.mult).then_inc(at_negmax, 1)
                    if g >= 1:
                        turned_out(g - 1)
                    for h in hooks[g]:
                        hook(h, prev, after)
                turned_out(groups - 1)
                dve.wait_ge(at_probs, G + groups)
                nc.vector.reciprocal(inv_sum[:, :, 0:heads], row_sum[:, :, 0:heads]).then_inc(at_inv, 1)
                dve.wait_ge(at_inv, A + 1)
                dve.wait_ge(at_tok, A + 1)
                for t in range(NT):
                    ins = nc.vector.tensor_tensor(normalised()[:, t * P:(t + 1) * P].rearrange("p (h s) -> p h s", h=heads),
                                                  bank[4][:, t * P:(t + 1) * P].rearrange("p (h s) -> p h s", h=heads),
                                                  inv_sum[:, t, 0:heads].rearrange("p (h o) -> p h o", o=1).broadcast_to([P, heads, D // heads]),
                                                  ALU.mult)
                ins.then_inc(at_norm, 1)
                if after is not None and joined(after):
                    values_out(after)
                dve.wait_ge(at_hi, A + 1)
                nc.vector.tensor_tensor(h_lo[:, 0, :], bank[5][:, :], h_hi[:, 0, :].bitcast(F32), ALU.subtract).then_inc(at_lo, 1)
                dve.wait_ge(at_y, A + 1)
                if heads > 1:
                    nc.vector.tensor_scalar(yT[:, :], bank[7][:, :], const("bo"), None, ALU.add).then_inc(yT_done, 1)
                else:
                    nc.vector.tensor_copy(yT[:, :], bank[7][:, :]).then_inc(yT_done, 1)
                for h in late_hooks:
                    hook(h, prev, after)

            dve.wait_ge(const_ready, 1)
            dve.wait_ge(consts_in, 16)
            dve.wait_ge(sel_in, 16)
            nc.vector.tensor_copy(sel1[:, :, :].rearrange("p e m -> p (e m)"),
                                  hidden[0:32, :, :].rearrange("p a n -> p (a n)")[:, 0:9 * P]).then_inc(sel_ready, 1)
            nc.vector.tensor_copy(ident_b[:, :], ident)
            nc.vector.tensor_copy(cmask_b[:, :], const("cmask"))
            nc.vector.tensor_copy(ones_r[:, :], ones[:, :]).then_inc(setup_done, 1)
            first = Job(0, 0, 0)
            for h in START:
                if isinstance(h, int):
                    first_piece(h)
                else:
                    hook(h, None, first)
            each_job(dve, main)
            last = Job(NL - 1, NC - 1, 1)
            hook("fin", last, None)

        @block.tensor
        def _(pe):
            def product(out, w, z, start, stop):
                (w_hi, w_lo), (a_hi, a_lo) = w, z
                nc.tensor.matmul(out, w_hi, a_hi, start=start, stop=False)
                nc.tensor.matmul(out, w_hi, a_lo, start=False, stop=False)
                return nc.tensor.matmul(out, w_lo, a_hi, start=False, stop=stop)

            def hook(h, prev, after):
                if h == "fin" and prev is not None:
                    if prev.y["kind"] == "ffn" and prev.y["route"]:
                        pe.wait_ge(added, prev.adds + prev.y["ne"] - 1)
                    else:
                        pe.wait_ge(yT_done, YT[prev.L] + prev.c + 1)
                    pe.wait_ge(zlo_done, prev.J + (3 if after is not None else 1 if job_is_last(prev) else 2))
                    if after is None:
                        pe.wait_ge(x_done, prev.J)
                    for t in range(NT):
                        ins = nc.tensor.transpose(turn_bank[:, t * P:(t + 1) * P], yT[:, t * P:(t + 1) * P], ident)
                    ins.then_inc(turned, 1)
                elif h == "zT":
                    pe.wait_ge(z_done, after.J + 1)
                    if after.y["kind"] == "retention" and not job_first(after):
                        pe.wait_ge(x_done, after.L * NC - (isinstance(after.c, int) and after.c == 1))
                    else:
                        wait(pe, x_done, after.J - 2)
                    for t in range(NT):
                        ins = nc.tensor.transpose(turn_bank[:, t * P:(t + 1) * P], z_tok[:, t, :], ident)
                    ins.then_inc(zT_done, 1)
                elif h == "logits":
                    pe.wait_ge(zlo_done, after.J + 1)
                    wait(pe, cT_done, after.R)
                    product(route_bank[:, :], router(after), z_of(after), True, True).then_inc(logits_done, 1)
                elif h == "back":
                    pe.wait_ge(const_ready, 1)
                    pe.wait_ge(lgT_done, after.R + 1)
                    for t in range(NT):
                        ins = nc.tensor.transpose(route_bank[:, t * P:(t + 1) * P], lgT[:, t * P:(t + 1) * P], ident)
                    ins.then_inc(back_done, 1)
                elif h == "cs":
                    pe.wait_ge(route_step, after.rsteps + R_STEPS[after.y["route"]])
                    for t in range(NT):
                        ins = nc.tensor.transpose(route_bank[0:32, t * P:(t + 1) * P], cs[:, t, :], ident)
                    ins.then_inc(csT_done, 1)

            def z_of(job):
                return z_hi[:, job.u, :], z_lo[:, job.u, :]

            def up(job, k):
                first_piece(job, k)
                wait(pe, act_done, tile_before(job, k))
                product(h_bank[slot(job, k)][:, :], weights(job, "w1", k), z_of(job), True, True).then_inc(up_done, 1)

            def first_piece(job, k):
                if job.L == 0 and isinstance(job.c, int) and job.c == 0 and k % 2 == 0:
                    pe.wait_ge(first_piece_split, 2 + k // 2)

            def gain_bc(job, e):
                wait(pe, gain_done, job.gains + e)
                nc.tensor.matmul(gain_bank[:, :], sel1[:, e, :], cT[:, job.u, :], start=True, stop=True).then_inc(gain_mm, 1)

            def down(job, k):
                per = job.y["n"] // job.y["ne"]
                e = k // per
                pe.wait_ge(lo_done, job.tiles + k + 1)
                if k % per == 0:
                    if job.y["route"]:
                        wait(pe, scaled_done, job.gains + e - 1)
                    else:
                        wait(pe, yT_done, YT[job.L] + job.c - 1)
                ins = product(y_bank[turn(job, e)][:, :], weights(job, "w2", k), (h_hi[:, slot(job, k), :], h_lo[:, slot(job, k), :]),
                              k % per == 0, k % per == per - 1)
                if k % per == per - 1:
                    ins.then_inc(y_done, 1)

            def main(job, prev, after):
                y = job.y
                pe.wait_ge(zlo_done, job.J + 1)
                if y["kind"] == "ffn":
                    per = y["n"] // y["ne"]
                    hooks = hooks_at(job, after, PE_AT)
                    if job.L and layers[job.L - 1]["kind"] != "ffn":
                        quiet(job)
                    if y["name"] == "ff3" and job_first(job):
                        pe.wait_ge(ternary_step, TERNARY_STEPS)
                    if not joined(job):
                        for k in range(3):
                            up(job, k)
                    if job.L == 0 and job_first(job):
                        hook("cs", None, job)
                    if y["route"]:
                        pe.wait_ge(cT_done, job.R + 1)
                    for k in range(y["n"]):
                        if y["route"] and k % per == 0:
                            gain_bc(job, k // per)
                        down(job, k)
                        if k + 3 < y["n"]:
                            up(job, k + 3)
                        elif after is not None and joined(after):
                            if not y["route"]:
                                tiles = ([], [], [0, 1, 2])
                            elif y["n"] % 3 != 0 and after.u == 0:
                                tiles = ([], [0], [1, 2])
                            else:
                                tiles = ([0], [1], [2])
                            for m in tiles[k + 3 - y["n"]]:
                                if m == 0:
                                    pe.wait_ge(zlo_done, after.J + 1)
                                up(after, m)
                        for h in hooks[k]:
                            hook(h, prev, after)
                elif y["kind"] == "pattention":
                    pattention(job, prev, after)
                elif y["kind"] == "attention":
                    if y["heads"] == 1 and isinstance(job.c, int) and job.c == 0:
                        pe.wait_ge(ternary_sum, 2)
                        wait(pe, cT_done, ROUTED[job.L])
                        nc.tensor.matmul(bank[7][:, 0:2], ones[:, :], w_size[:, 0:2], start=True, stop=True).then_inc(ternary_total, 1)
                    attention(job, prev, after)
                elif y["kind"] == "glu":
                    glu(job, prev, after)
                elif y["kind"] == "retention":
                    retention(job, prev, after)

            def retention(job, prev, after):
                c = job.c
                quiet(job)
                wait(pe, rt_kv, c)
                wait(pe, rt_queries, c)
                product(bank[0][:, :], late("wk3"), z_of(job), True, True).then_inc(rt_proj, 1)
                product(bank[1][:, :], late("wv3"), z_of(job), True, True).then_inc(rt_proj, 1)
                product(bank[2][:, :], late("wq3"), z_of(job), True, True).then_inc(rt_proj, 1)
                within, at_end = retention_hooks(job, after)
                for h in within:
                    hook(h, prev, after)
                pe.wait_ge(rt_vlo, c + 1)
                nc.tensor.matmul(bank[3][:, :], ones_r[:, :], h_hi[:, 0, :], start=True, stop=False)
                nc.tensor.matmul(bank[3][:, :], ones_r[:, :], h_lo[:, 0, :], start=False, stop=True).then_inc(rt_vsum, 1)
                if isinstance(c, int) and c == NC - 1:
                    pe.wait_ge(rt_states, 1)
                    for u in range(2):
                        ins = nc.tensor.transpose(bank[0][:, u * P:(u + 1) * P], states[:, u:T:2], ident)
                    ins.then_inc(rt_states_t, 1)
                    pe.wait_ge(zlo_done, job.J + 1)
                    with pe.Fori(0, NC) as i:
                        pe.wait_ge(yT_done, i + (YT[job.L] + 1))
                        pe.wait_ge(x_done, i + job.L * NC)
                        for t in range(NT):
                            ins = nc.tensor.transpose(turn_bank[:, t * P:(t + 1) * P], yT[:, t * P:(t + 1) * P], ident)
                        ins.then_inc(turned, 1)
                for h in at_end:
                    hook(h, prev, after)

            def quiet(job):
                if isinstance(job.c, int) and job.c == 0:
                    before_ = layers[job.L - 1]
                    if before_["kind"] == "ffn" and before_["route"]:
                        pe.wait_ge(scaled_done, GAINS[job.L])
                        pe.wait_ge(added, ADDS[job.L])
                    else:
                        wait(pe, yT_done, YT[job.L])

            def z_tile(job, t):
                return z_hi[:, job.u, t * P:(t + 1) * P], z_lo[:, job.u, t * P:(t + 1) * P]

            def pattention(job, prev, after):
                n0 = PATS[job.L] + job.c
                hooks = spread(hook_names(after), 6)
                if isinstance(job.c, int) and job.c == 0:
                    pe.wait_ge(first_piece_split, len(FIRST))
                quiet(job)
                wait(pe, yT_done, YT[job.L] + job.c)
                out = pat_out(after)

                def logits(job):
                    for t in range(NT):
                        product(bank[t][:, :], z_tile(job, t), small("key"), True, True).then_inc(pa_logits, 1)

                def down(k):
                    pe.wait_ge(pa_lo, n0 * NT + k + 1)
                    ins = product(out[:, :], small("value", k * P, (k + 1) * P), (h_hi[:, k % 3, :], h_lo[:, k % 3, :]), k == 0, k == 3)
                    if k == 3:
                        ins.then_inc(pa_y, 1)

                if not joined(job):
                    wait(pe, cT_done, ROUTED[job.L])
                    logits(job)
                for i in range(2):
                    for h in hooks[i]:
                        hook(h, prev, after)
                for k in range(4):
                    pe.wait_ge(pa_gelu, n0 * NT + NT)
                    if k >= 2:
                        pe.wait_ge(pa_lo, n0 * NT + k - 1)
                    else:
                        wait(pe, pa_lo, n0 * NT)
                    for t in range(NT):
                        ins = nc.tensor.transpose(bank[4 + k % 2][:, t * P:(t + 1) * P], pat_rows(t)[:, k * P:(k + 1) * P], ident)
                    ins.then_inc(pa_turned, 1)
                    if k >= 1:
                        down(k - 1)
                    for h in hooks[2 + k]:
                        hook(h, prev, after)
                if after is not None and joined(after):
                    pe.wait_ge(zlo_done, after.J + 1)
                    logits(after)
                down(3)

            def glu(job, prev, after):
                n = job.y["n"]
                n0 = PAIRS[job.L] + job.c * n
                hooks = hooks_at(job, after, None)
                quiet(job)
                pe.wait_ge(cT_done, job.R + 1)

                def pair(job, k):
                    wait(pe, glu_uv, PAIRS[job.L] + job.c * n + k - 1)
                    product(glu_bank(0, k)[:, :], late("gate", k * P, (k + 1) * P), z_of(job), True, True)
                    product(glu_bank(1, k)[:, :], late("up", k * P, (k + 1) * P), z_of(job), True, True).then_inc(glu_mm, 1)

                def weigh(job, k):
                    wait(pe, gain_done, job.gains + k)
                    sel = late("sel2", k * P, (k + 1) * P)[0]
                    nc.tensor.matmul(gain_bank[:, :], sel[0:32, :], cT[:, job.u, :], start=True, stop=True).then_inc(gain_mm, 1)

                if not joined(job):
                    pair(job, 0)
                    weigh(job, 0)
                    pair(job, 1)
                weigh(job, 1)
                for k in range(n):
                    if k + 2 < n:
                        pair(job, k + 2)
                        weigh(job, k + 2)
                    pe.wait_ge(glu_lo, n0 + k + 1)
                    if k == 0:
                        wait(pe, yT_done, YT[job.L] + job.c)
                    ins = product(bank[4][:, :], late("down", k * P, (k + 1) * P), (h_hi[:, k % 3, :], h_lo[:, k % 3, :]), k == 0, k == n - 1)
                    if k == n - 1:
                        ins.then_inc(glu_y, 1)
                    for h in hooks[k]:
                        hook(h, prev, after)
                    if k + 2 >= n and after is not None and joined(after):
                        if k + 2 == n:
                            pe.wait_ge(zlo_done, after.J + 1)
                            pair(after, 0)
                        else:
                            pe.wait_ge(cT_done, after.R + 1)
                            weigh(after, 0)
                            pair(after, 1)

            def attention(job, prev, after):
                y = job.y
                heads, per = y["heads"], y["per"]
                groups = SEQ * heads // per
                A = ATTS[job.L] + job.c
                G = GROUPS[job.L] + job.c * groups
                hooks, late_hooks = attention_hooks(job, after)
                values, turned_p = attention_buffers(job)
                w = small if heads > 1 else late
                n = "1" if heads > 1 else "2"

                def queries_keys(job):
                    pe.wait_ge(zlo_done, job.J + 1)
                    product(bank[0][:, :], w("wq" + n), z_of(job), True, True).then_inc(at_proj, 1)
                    product(bank[1][:, :], w("wk" + n), z_of(job), True, True).then_inc(at_proj, 1)

                def values_of(job):
                    for t in range(NT):
                        ins = product(bank[2][:, t * P:(t + 1) * P], z_tile(job, t), w("wv" + n), True, True)
                    ins.then_inc(at_proj, 1)

                def scores(job, g):
                    b = g // (groups // SEQ)
                    A = ATTS[job.L] + job.c
                    G = GROUPS[job.L] + job.c * groups
                    if heads > 1:
                        pe.wait_ge(at_keys, G - GROUPS[job.L] + g + 1)
                        keys = gain[:, g % 2, :].rearrange("p (h t) -> p h t", h=per)
                    else:
                        keys = scaled[:, 1, b * T:(b + 1) * T].rearrange("p (h t) -> p h t", h=1)
                    wait(pe, at_probs, G + g - 1)
                    if g == 0:
                        pe.wait_ge(at_qk, A * 2 + 2)
                    if g == 1:
                        pe.wait_ge(at_v, A + 1)
                    for qb in range(2):
                        out = bank[2 * (g % 2) + qb][:, 0:per * (qb + 1) * P].rearrange("p (h k) -> p h k", h=per)
                        q = scaled[:, 0, b * T + qb * P:b * T + (qb + 1) * P]
                        nc.tensor.matmul(out, q, keys[:, :, 0:(qb + 1) * P], start=True, stop=False, skip_group_check=True)
                        ins = nc.tensor.matmul(out[:, :, qb * P:(qb + 1) * P], ident_b[:, :],
                                               cmask_b[:, :].rearrange("p (o k) -> p o k", o=1).broadcast_to([P, per, P]),
                                               start=False, stop=True, skip_group_check=True)
                    ins.then_inc(at_scores, 1)

                def turn(g):
                    pe.wait_ge(at_probs, G + g + 1)
                    wait(pe, at_out_a, G + g)
                    wait(pe, at_out_d, G + g)
                    probs = hidden[:, :, :].rearrange("p a n -> p (a n)").rearrange("p (s n) -> p s n", s=2)[:, g % 2, :]
                    for h in range(per):
                        nc.tensor.transpose(bank[4][:, 2 * h * P:(2 * h + 1) * P], probs[:, h * P:(h + 1) * P], ident)
                        at = per * P + h * 2 * P
                        nc.tensor.transpose(bank[4][:, (2 * h + 1) * P:(2 * h + 2) * P], probs[:, at:at + P], ident)
                        ins = nc.tensor.transpose(bank[5][:, h * P:(h + 1) * P], probs[:, at + P:at + 2 * P], ident)
                    ins.then_inc(at_turned, 1)

                def weigh(g):
                    b, hp = g // (groups // SEQ), g % (groups // SEQ)
                    if g == 0:
                        wait(pe, yT_done, YT[job.L] + job.c)
                    pe.wait_ge(at_out_a, G + g + 1)
                    pe.wait_ge(at_out_d, G + g + 1)
                    for h in range(per):
                        at = (hp * per + h) * D
                        head = hp * per + h
                        nc.tensor.matmul(bank[7][:, b * T:(b + 1) * T], values[:, 2 * b, at:at + D],
                                         turned_p[:, g % 2, 2 * h * P:(2 * h + 2) * P],
                                         start=head == 0, stop=False, skip_group_check=True)
                        ins = nc.tensor.matmul(bank[7][:, b * T + P:(b + 1) * T], values[:, 2 * b + 1, at:at + D],
                                               turned_p[:, g % 2, (2 * per + h) * P:(2 * per + h + 1) * P],
                                               start=False, stop=head == heads - 1, skip_group_check=True)
                    ins.then_inc(at_pv, 1)

                if not joined(job):
                    quiet(job)
                    wait(pe, cT_done, job_routed(job))
                    queries_keys(job)
                    values_of(job)
                    pe.wait_ge(setup_done, 1)
                    pe.wait_ge(at_v, A + 1)
                    scores(job, 0)
                for g in range(groups):
                    if g + 1 < groups and not (g == 0 and joined(job)):
                        scores(job, g + 1)
                    turn(g)
                    if g >= 1:
                        weigh(g - 1)
                    for h in hooks[g]:
                        hook(h, prev, after)
                follow = after is not None and joined(after)
                if follow:
                    queries_keys(after)
                weigh(groups - 1)
                if follow:
                    values_of(after)
                pe.wait_ge(at_raw, A + 1)
                for t in range(NT):
                    ins = nc.tensor.transpose(bank[4][:, t * P:(t + 1) * P], yT[:, t * P:(t + 1) * P], ident)
                ins.then_inc(at_tok, 1)
                if follow:
                    scores(after, 0)
                pe.wait_ge(at_norm, A + 1)
                for t in range(NT):
                    ins = nc.tensor.transpose(bank[5][:, t * P:(t + 1) * P], normalised()[:, t * P:(t + 1) * P], ident)
                ins.then_inc(at_back, 1)
                if follow:
                    scores(after, 1)
                pe.wait_ge(at_lo, A + 1)
                product(bank[7][:, :], w("wo" + n), (h_hi[:, 0, :], h_lo[:, 0, :]), True, True).then_inc(at_y, 1)
                if late_hooks:
                    pe.wait_ge(yT_done, YT[job.L] + job.c + 1)
                for h in late_hooks:
                    hook(h, prev, after)

            def job_routed(job):
                return ROUTED[job.L]

            pe.wait_ge(consts_in, 16)
            pe.wait_ge(sel_ready, 1)
            first = Job(0, 0, 0)
            hook("zT", None, first)
            pe.wait_ge(first_piece_split, 1)
            for h in ("logits", "back"):
                hook(h, None, first)
            each_job(pe, main)
            hook("fin", Job(NL - 1, NC - 1, 1), None)


def kernel(**inputs):
    import concourse.bacc as _bacc
    from concourse.bass_utils import run_bass_kernel_spmd as _run

    nc = _bacc.Bacc("TRN2", target_bir_lowering=False, num_devices=1)
    arrays = lay_out({k: np.asarray(v) for k, v in inputs.items()})
    args = [nc.dram_tensor(n, a.shape, F32, kind="ExternalInput").ap() for n, a in arrays.items()]
    args.append(nc.dram_tensor("x_out", (B, T, D), F32, kind="ExternalOutput").ap())
    twelve_sublayers(nc, *args)
    r = _run(nc, [arrays], core_ids=[0])
    return r.results[0]["x_out"]


def lay_out(i):
    def hidden_tiles(w):
        w = w.reshape(-1, P, D)
        return w.transpose(1, 0, 2).reshape(P, -1)

    w1, w2 = i["L0_ffn_w1"], i["L0_ffn_w2"]
    w0 = np.concatenate([a for e in range(8) for a in (w1[e].T, hidden_tiles(w2[e].T))], axis=1)
    zero = np.zeros((P, P), np.float32)

    def router(*ws):
        w = np.concatenate(ws, axis=1)
        return np.concatenate([w, zero[:, w.shape[1]:]], axis=1)

    ws = np.concatenate([router(i["L0_ffn_router_w"].T), router(i["L1_ffn_Wg"], i["L1_ffn_Wr"]),
                         i["L0_attn_key_param_tokens"].T, hidden_tiles(i["L0_attn_value_param_tokens"]),
                         i["L1_attn_Wq"].T, i["L1_attn_Wk"].T, i["L1_attn_Wv"].T, i["L1_attn_Wo"].T], axis=1)
    wb = np.concatenate([i["L1_ffn_W1"].transpose(1, 0, 2).reshape(P, -1), i["L1_ffn_D1"],
                         hidden_tiles(i["L1_ffn_W2"]), hidden_tiles(i["L1_ffn_D2"])], axis=1)
    sel2 = np.zeros((P, 8, P), np.float32)
    for r in range(32):
        e = r % 16
        sel2[r, e // 2, 64 * (e % 2):64 * (e % 2) + 64] = 1.0
    wa = np.concatenate([i["L2_ffn_w_gate"].transpose(2, 0, 1).reshape(P, -1),
                         i["L2_ffn_w_up"].transpose(2, 0, 1).reshape(P, -1),
                         hidden_tiles(i["L2_ffn_w_down"].transpose(0, 2, 1)), router(i["L2_ffn_router_weight"].T),
                         sel2.reshape(P, -1), i["L2_attn_Wq"], i["L2_attn_Wk"], i["L2_attn_Wv"], i["L2_attn_Wo"],
                         i["L3_attn_Wq"], i["L3_attn_Wk"], i["L3_attn_Wv"], zero], axis=1)
    w3 = np.concatenate([i["L3_ffn_W1"].T, hidden_tiles(i["L3_ffn_W2"].T)], axis=1)

    cst = {n: np.zeros((P, w), np.float32) for n, (_, w) in C_COLS.items()}
    cst["ident"] = np.eye(P, dtype=np.float32)
    sel1 = np.zeros((32, 9, P), np.float32)
    for e in range(9):
        sel1[e, e] = sel1[16 + e, e] = 1.0
    cst["iota"][:] = np.arange(16, dtype=np.float32)
    cst["bias2"][:] = i["L2_ffn_router_bias"]
    cst["b1_0"][:] = i["L0_ffn_b1"].reshape(-1, P).T
    cst["b2_0"][:] = i["L0_ffn_b2"].T
    cst["b1_1"][:, 0:32] = i["L1_ffn_b1"].reshape(-1, P).T
    cst["b1_1"][:, 32:36] = i["L1_ffn_d1b"].reshape(-1, P).T
    cst["b2_1"][:, 0:8] = i["L1_ffn_b2"].T
    cst["b2_1"][:, 8] = i["L1_ffn_d2b"]
    cst["b1_3"][:] = i["L3_ffn_b1"].reshape(-1, P).T
    cst["b2_3"][:, 0] = i["L3_ffn_b2"]
    cst["rb1"][0:8, 0] = i["L1_ffn_bg"]
    cst["rb1"][8:10, 0] = i["L1_ffn_br"]
    cst["bq"][:, 0] = i["L1_attn_bq"]
    cst["bk"][:, 0] = i["L1_attn_bk"]
    cst["bo"][:, 0] = i["L1_attn_bo"]
    cst["bv"][:] = i["L1_attn_bv"]
    for h in range(HEADS):
        cst["hmask"][h * HD:(h + 1) * HD, h] = 1.0
    rows = np.arange(P)
    cst["cmask"][:] = np.where(rows[None, :] > rows[:, None], np.float32(LOWEST), np.float32(0.0))
    out = {"x": i["L0_attn_inputs"], "w0": w0, "ws": ws, "wb": wb, "wa": wa, "w3": w3,
           "cst": np.concatenate([cst[n] for n in C_COLS], axis=1), "sel": sel1.reshape(32, -1)}
    return {f"in_{k}": np.ascontiguousarray(v) for k, v in out.items()}
```
